# Optimizing a Trainium2 kernel written in Bass

```python
import numpy as np
import jax
import jax.numpy as jnp

def _softmax(x, axis=-1):
    return jax.nn.softmax(x, axis=axis)

def _gelu(x):
    return jax.nn.gelu(x, approximate=True)

def _silu(x):
    return jax.nn.silu(x)

def _sigmoid(x):
    return jax.nn.sigmoid(x)

def _layernorm(x, axis=-1, eps=1e-05):
    m = jnp.mean(x, axis=axis, keepdims=True)
    v = jnp.var(x, axis=axis, keepdims=True)
    return (x - m) / jnp.sqrt(v + eps)

def _scatter_add(tgt, idx, src, axis=0):
    return tgt.at[idx].add(src)

def _segment_sum(src, seg, n):
    return jax.ops.segment_sum(src, seg, n)
kernel_name = 'mk_adaln_ffn_d2_seqx_r8_e51625'

def setup_inputs(seed: int=0):
    np.random.seed(seed)
    _w = jnp.asarray

    def _rec_inputs():
        import jax
        import jax.numpy as jnp
        _rk = jax.random.key(seed)
        x = -7.109e-05 + 0.9999 * jax.random.normal(jax.random.fold_in(_rk, 1), (128, 32, 512), jnp.float32)
        _lenS = 32 - jax.random.randint(jax.random.fold_in(_rk, 7), (128,), 0, max(1, 32 // 4) + 1, jnp.int32)
        _lenS2 = 32 - jax.random.randint(jax.random.fold_in(_rk, 8), (128,), 0, max(1, 32 // 4) + 1, jnp.int32)
        itok_B_0_15 = jax.random.randint(jax.random.fold_in(_rk, 11), (128,), 0, 16, jnp.int32)
        itok_B_3_7 = jax.random.randint(jax.random.fold_in(_rk, 12), (128,), 3, 8, jnp.int32)
        return (x, itok_B_0_15, itok_B_3_7)
    x, itok_B_0_15, itok_B_3_7 = _rec_inputs()

    def _L0_cond_setup():
        import jax, jax.numpy as jnp
        import numpy as np
        NUM_CONDITIONS = 16
        IN_CH = 32
        OUT_CH = 32
        B = 64
        T = 512
        key = jax.random.key(seed)
        k_x, k_w, k_c = jax.random.split(key, 3)
        x = jax.random.normal(k_x, (B, IN_CH, T), dtype=jnp.float32)
        bound = float(np.sqrt(6.0 / IN_CH))
        weights = jax.random.uniform(k_w, (NUM_CONDITIONS, IN_CH, OUT_CH), dtype=jnp.float32, minval=-bound, maxval=bound)
        condition = jax.random.randint(k_c, (B,), 0, NUM_CONDITIONS, dtype=jnp.int64)
        return {'x': x, 'weights': weights, 'condition': condition}
    _L0_cond_all = _L0_cond_setup()
    _L0_cond_in = {k: v for k, v in _L0_cond_all.items() if k in ('weights',)}
    del _L0_cond_all

    def _L0_ffn_setup():
        import jax, jax.numpy as jnp
        import numpy as np
        BATCH, TOK, DIM, OUT = (4, 256, 512, 512)
        E, R, TOP_K = (8, 16, 2)
        SCALING = 16.0 / R
        key = jax.random.key(seed)
        ks = jax.random.split(key, 6)
        return {'x': jax.random.normal(ks[0], (BATCH, TOK, DIM), dtype=jnp.float32), 'W_base': jax.random.normal(ks[1], (OUT, DIM), dtype=jnp.float32) / np.sqrt(DIM), 'b_base': jax.random.normal(ks[2], (OUT,), dtype=jnp.float32) * 0.01, 'W_gate': jax.random.normal(ks[3], (E, DIM), dtype=jnp.float32) * 0.01, 'A': jax.random.normal(ks[4], (E, R, DIM), dtype=jnp.float32) / np.sqrt(DIM), 'B': jax.random.normal(ks[5], (OUT, OUT // OUT * R * 0 + R), dtype=jnp.float32)[None].repeat(E, 0) * 0.0 + jax.random.normal(ks[5], (E, OUT, R), dtype=jnp.float32) * 0.02}
    _L0_ffn_all = _L0_ffn_setup()
    _L0_ffn_in = {k: v for k, v in _L0_ffn_all.items() if k in ('W_base', 'b_base', 'W_gate', 'A', 'B')}
    del _L0_ffn_all

    def _L1_cond_setup():
        import jax, jax.numpy as jnp
        import numpy as np
        RANK = 16
        ALPHA = 16.0
        SCALING = ALPHA / RANK
        N_ADAPTERS = 8
        IN_F = 512
        OUT_F = 512
        BATCH = 4
        SEQ = 256
        key = jax.random.key(seed)
        kx, ka, kb, ki = jax.random.split(key, 4)
        x = jax.random.normal(kx, (BATCH, SEQ, IN_F), dtype=jnp.float32)
        A = jax.random.normal(ka, (N_ADAPTERS, OUT_F, RANK), dtype=jnp.float32) * 0.02
        B = jax.random.normal(kb, (N_ADAPTERS, RANK, IN_F), dtype=jnp.float32) * 0.02
        adapter_ids = jax.random.randint(ki, (BATCH,), 0, N_ADAPTERS, dtype=jnp.int32)
        return {'x': x, 'A': A, 'B': B, 'adapter_ids': adapter_ids}
    _L1_cond_all = _L1_cond_setup()
    _L1_cond_in = {k: v for k, v in _L1_cond_all.items() if k in ('A', 'B')}
    del _L1_cond_all

    def _L1_ffn_setup():
        import jax, jax.numpy as jnp
        import numpy as np
        H = 512
        I = 256
        E = 16
        TOPK = 4
        SI = 256
        key = jax.random.key(seed)
        ks = jax.random.split(key, 9)
        s = 0.02
        return {'hidden_states': jax.random.normal(ks[0], (2, 256, H), dtype=jnp.float32), 'gate_w': jax.random.normal(ks[1], (E, H), dtype=jnp.float32) * s, 'bias': jnp.zeros((E,), dtype=jnp.float32), 'Wg': jax.random.normal(ks[2], (E, I, H), dtype=jnp.float32) * s, 'Wu': jax.random.normal(ks[3], (E, I, H), dtype=jnp.float32) * s, 'Wd': jax.random.normal(ks[4], (E, H, I), dtype=jnp.float32) * s, 'Sg': jax.random.normal(ks[5], (SI, H), dtype=jnp.float32) * s, 'Su': jax.random.normal(ks[6], (SI, H), dtype=jnp.float32) * s, 'Sd': jax.random.normal(ks[7], (H, SI), dtype=jnp.float32) * s}
    _L1_ffn_all = _L1_ffn_setup()
    _L1_ffn_in = {k: v for k, v in _L1_ffn_all.items() if k in ('gate_w', 'bias', 'Wg', 'Wu', 'Wd', 'Sg', 'Su', 'Sd')}
    del _L1_ffn_all
    return {'x': x, 'itok_B_0_15': itok_B_0_15, 'itok_B_3_7': itok_B_3_7, 'L0_cond_weights': _L0_cond_in['weights'], 'L0_ffn_W_base': _L0_ffn_in['W_base'], 'L0_ffn_b_base': _L0_ffn_in['b_base'], 'L0_ffn_W_gate': _L0_ffn_in['W_gate'], 'L0_ffn_A': _L0_ffn_in['A'], 'L0_ffn_B': _L0_ffn_in['B'], 'L1_cond_A': _L1_cond_in['A'], 'L1_cond_B': _L1_cond_in['B'], 'L1_ffn_gate_w': _L1_ffn_in['gate_w'], 'L1_ffn_bias': _L1_ffn_in['bias'], 'L1_ffn_Wg': _L1_ffn_in['Wg'], 'L1_ffn_Wu': _L1_ffn_in['Wu'], 'L1_ffn_Wd': _L1_ffn_in['Wd'], 'L1_ffn_Sg': _L1_ffn_in['Sg'], 'L1_ffn_Su': _L1_ffn_in['Su'], 'L1_ffn_Sd': _L1_ffn_in['Sd']}

def reference(x, itok_B_0_15, itok_B_3_7, L0_cond_weights, L0_ffn_W_base, L0_ffn_b_base, L0_ffn_W_gate, L0_ffn_A, L0_ffn_B, L1_cond_A, L1_cond_B, L1_ffn_gate_w, L1_ffn_bias, L1_ffn_Wg, L1_ffn_Wu, L1_ffn_Wd, L1_ffn_Sg, L1_ffn_Su, L1_ffn_Sd):
    import jax
    import jax.numpy as jnp

    def _L0_cond_ref(x, weights, condition):
        import jax, jax.numpy as jnp
        import numpy as np
        NUM_CONDITIONS = 16
        IN_CH = 32
        OUT_CH = 32
        B = 64
        T = 512
        W = weights[condition]
        return jnp.einsum('bct,bcd->bdt', x, W)

    def _L0_ffn_ref(x, W_base, b_base, W_gate, A, B):
        import jax, jax.numpy as jnp
        import numpy as np
        BATCH, TOK, DIM, OUT = (4, 256, 512, 512)
        E, R, TOP_K = (8, 16, 2)
        SCALING = 16.0 / R
        result = jnp.einsum('bnd,od->bno', x, W_base) + b_base
        logits = jnp.einsum('bnd,ed->bne', x, W_gate)
        probs = jax.nn.softmax(logits.astype(jnp.float32), axis=-1)
        top_p, top_i = jax.lax.top_k(probs, TOP_K)
        top_p = top_p / jnp.sum(top_p, axis=-1, keepdims=True)
        top_p = top_p.astype(x.dtype)
        route_w = jnp.sum(jax.nn.one_hot(top_i, E, dtype=x.dtype) * top_p[..., None], axis=-2)
        h = jnp.einsum('bnd,erd->bner', x, A)
        hw = h * route_w[..., None]
        delta = jnp.einsum('bner,eor->bno', hw, B)
        return result + delta * SCALING

    def _L1_cond_ref(x, A, B, adapter_ids):
        import jax, jax.numpy as jnp
        import numpy as np
        RANK = 16
        ALPHA = 16.0
        SCALING = ALPHA / RANK
        N_ADAPTERS = 8
        IN_F = 512
        OUT_F = 512
        BATCH = 4
        SEQ = 256
        B_sel = B[adapter_ids]
        A_sel = A[adapter_ids]
        Bx = jnp.einsum('bni,bri->bnr', x, B_sel)
        out = jnp.einsum('bnr,bor->bno', Bx, A_sel)
        return out * SCALING

    def _L1_ffn_ref(hidden_states, gate_w, bias, Wg, Wu, Wd, Sg, Su, Sd):
        import jax, jax.numpy as jnp
        import numpy as np
        H = 512
        I = 256
        E = 16
        TOPK = 4
        SI = 256
        orig_shape = hidden_states.shape
        x = hidden_states.reshape(-1, orig_shape[-1])
        scores = jax.nn.sigmoid(x @ gate_w.T) + bias
        topk_w, topk_idx = jax.lax.top_k(scores, TOPK)
        topk_w = topk_w / (jnp.sum(topk_w, axis=-1, keepdims=True) + 1e-20)
        cw = jnp.sum(jax.nn.one_hot(topk_idx, E, dtype=x.dtype) * topk_w[..., None], axis=1)
        g = jnp.einsum('th,eih->eti', x, Wg)
        u = jnp.einsum('th,eih->eti', x, Wu)
        z = jax.nn.silu(g) * u
        zw = z * cw.T[:, :, None]
        out = jnp.einsum('eti,ehi->th', zw, Wd)
        out = out + jax.nn.silu(x @ Sg.T) * (x @ Su.T) @ Sd.T
        return out.reshape(orig_shape)
    x = x + _L0_ffn_ref(_L0_cond_ref(x, L0_cond_weights, itok_B_0_15), L0_ffn_W_base, L0_ffn_b_base, L0_ffn_W_gate, L0_ffn_A, L0_ffn_B)
    x = x + _L1_ffn_ref(_L1_cond_ref(x, L1_cond_A, L1_cond_B, itok_B_3_7), L1_ffn_gate_w, L1_ffn_bias, L1_ffn_Wg, L1_ffn_Wu, L1_ffn_Wd, L1_ffn_Sg, L1_ffn_Su, L1_ffn_Sd)
    return x

_drawn_inputs = setup_inputs


def setup_inputs(seed=0):
    import zlib

    import numpy as np

    out = dict(_drawn_inputs(seed))
    spreads = {'L1_ffn_bias': (0.0, 0.8)}
    factors = {'L0_ffn_b_base': 8.0,
     'L1_cond_A': 8.0,
     'L1_cond_B': 8.0,
     'L1_ffn_gate_w': 8.0,
     'L1_ffn_Wg': 8.0,
     'L1_ffn_Wu': 8.0,
     'L1_ffn_Wd': 8.0,
     'L1_ffn_Sg': 8.0,
     'L1_ffn_Su': 8.0,
     'L1_ffn_Sd': 8.0}
    for name, (base, spread) in spreads.items():
        noise = np.random.default_rng([zlib.crc32(name.encode()), seed]).standard_normal(out[name].shape)
        drawn = base * np.exp(spread * noise) if base else spread * noise
        out[name] = jnp.asarray(drawn.astype(out[name].dtype))
    for name, factor in factors.items():
        out[name] = (out[name] * factor).astype(out[name].dtype)
    return out
```

```python
from contextlib import ExitStack

import concourse.bass as bass
from concourse import mybir

F32 = mybir.dt.float32
I32 = mybir.dt.int32
U32 = mybir.dt.uint32
ALU = mybir.AluOpType
ACT = mybir.ActivationFunctionType
AX = mybir.AxisListType

P = 128
BATCH, SEQ, D = 128, 32, 512
TOK = BATCH * SEQ
NT = TOK // P
BPT = P // SEQ
KC = D // P
E0, K0, R = 8, 2, 16
E1, K1, I1 = 16, 4, 256
IC = I1 // P
NE = E1 + 1
NA = 8
GU = 2 * I1
REGION = TOK + P
SPARE = E1
NS = TOK * K1 // P + SPARE
ROWS = E1 * REGION + SPARE * P
U = 4


def adaln_ffn_kernel(nc, x, cond, adapters, cond_w, base_w, base_b, gate_lora0, lora_b0, adapter_b,
                     adapter_a, gate1, bias1, gate_up, down, out):
    q_rows = nc.dram_tensor("q_rows", [ROWS, P], F32).ap()
    y_rows = nc.dram_tensor("y_rows", [NS * P, D], F32).ap()
    x1_dram = nc.dram_tensor("x1_dram", [TOK, D], F32).ap()
    xr = x.rearrange("b s d -> (b s) d")
    outr = out.rearrange("b s d -> (b s) d")

    with ExitStack() as ctx:
        def sb(name, shape, dt=F32):
            return ctx.enter_context(nc.sbuf_tensor(name, shape, dt))

        def sem(name):
            return ctx.enter_context(nc.semaphore(name))

        bank = [ctx.enter_context(nc.psum_tensor(f"bank{i}", [P, 512], F32)) for i in range(8)]

        ident = sb("ident", [P, P])
        ones = sb("ones", [P, P])
        tri = sb("tri", [P, P])
        diag = sb("diag", [P, BPT, SEQ])
        iota_e = sb("iota_e", [P, E1])
        iota_a = sb("iota_a", [P, NA, R])
        zero_rows = sb("zero_rows", [P, P])
        part_i = sb("part_i", [P, 1], I32)
        part_f = sb("part_f", [P, 1])
        region_f = sb("region_f", [P, E1])
        cond_i = sb("cond_i", [P, NT], I32)
        cond_row = sb("cond_row", [P, NT], U32)
        c_i = sb("c_i", [P, 1], I32)
        c_f = sb("c_f", [P, 1])
        adapter_i = sb("adapter_i", [P, NT], I32)
        adapter_f = sb("adapter_f", [P, NT])
        base_w_sb = sb("base_w_sb", [P, KC, D])
        base_b_sb = sb("base_b_sb", [P, D])
        gl0_sb = sb("gl0_sb", [P, KC, E0 + E0 * R])
        lb0_sb = sb("lb0_sb", [P, D])
        ab_sb = sb("ab_sb", [P, KC, NA * R])
        aa_sb = sb("aa_sb", [P, KC, NA * R])
        g1_sb = sb("g1_sb", [P, KC, E1])
        gate_q = sb("gate_q", [P, E1])
        bias_sb = sb("bias_sb", [P, E1])
        stage = sb("stage", [P, 2, KC, GU])
        m_all = sb("m_all", [P, NE, GU])
        wd_all = sb("wd_all", [P, NE, IC, D])
        qT_all = sb("qT_all", [P, NT, P])

        xt = sb("xt", [P, U, D])
        xb = sb("xb", [P, 2, D])
        cidx = sb("cidx", [P, U], U32)
        wrow = sb("wrow", [P, U, SEQ])
        bd = sb("bd", [P, 2, BPT, SEQ])
        yT = sb("yT", [P, KC, P])
        hw = sb("hw", [P, E0, R])
        hwT = sb("hwT", [P, P])
        x1 = sb("x1", [P, 4, D])
        x1T = sb("x1T", [P, KC, P])
        q_sb = sb("q_sb", [P, U, NA, R])
        qT = sb("qT", [P, P])
        slot_i = sb("slot_i", [P, U, K1], U32)
        slots = sb("slots", [P, NT, K1])
        y_slots = sb("y_slots", [P, NT, K1], U32)
        w_all = sb("w_all", [P, NT, K1])
        chosen = sb("chosen", [P, NT, K1])
        r0 = sb("r0", [P, 96])
        r0i = sb("r0i", [P, 8], U32)
        r1 = sb("r1", [P, 96])
        r1i = sb("r1i", [P, 8], U32)
        oh = sb("oh", [P, K1, E1])
        ohr = sb("ohr", [P, K1, E1])
        mask = sb("mask", [P, 2, E1])
        rk = sb("rk", [P, E1])
        rowno = sb("rowno", [P, E1])
        slot_f = sb("slot_f", [P, K1])

        tf = sb("tf", [P, 6, E1])
        ti = sb("ti", [P, 2, E1], I32)
        pad_i = sb("pad_i", [P, E1], U32)
        iota_s = sb("iota_s", [P, NS])
        ge = sb("ge", [P, NS, E1])
        ts = sb("ts", [P, 4, NS])
        shift = sb("shift", [P, NT])
        tile_e = sb("tile_e", [1, NS], I32)
        tile_row = sb("tile_row", [1, NS], I32)

        s = {n: sem(n) for n in (
            "consts", "weights0", "wd_loaded", "gate_q_mm", "gate_q_ready", "bd_ready", "xb_ready", "yT_mm",
            "yT_ready", "h_mm", "d_ready", "exp0", "r0_step", "hw_ready", "hwT_mm", "hwT_ready", "r_mm",
            "x1_ready", "x1T_mm", "x1T_ready", "q_mm", "q_ready", "qT_mm", "qT_ready", "s_mm", "exp1",
            "r1_step", "mask_ready", "rank_mm", "rank_step", "slots_ready", "rank_done", "ci_ready",
            "m_mm", "m_ready", "t_step", "pad_ready", "tables", "pads", "spare_zero",
            "qs_mm", "qs_ready", "gu_mm", "silu_done", "z_ready", "zT_mm", "zT_ready", "y_mm", "y_sb",
            "ident0", "idx0", "cond_row", "acc_step", "out_ready", "gi_ready", "g1mm", "sh_y",
            "dve_held", "pool_held")}
        x_in = [sem(f"x_in{i}") for i in range(U)]
        w_in = [sem(f"w_in{i}") for i in range(U)]
        x1_out = [sem(f"x1_out{i}") for i in range(4)]
        scat = [sem(f"scat{i}") for i in range(U)]
        st_in = [sem(f"st_in{i}") for i in range(2)]
        qs_in = [sem(f"qs_in{i}") for i in range(2)]
        y_out = [sem(f"y_out{i}") for i in range(2)]
        g_in = [sem(f"g_in{i}") for i in range(2)]
        xc_in = [sem(f"xc_in{i}") for i in range(2)]
        o_out = [sem(f"o_out{i}") for i in range(2)]

        qs = xt[:, 0:2, 0:P]
        qsT = xt[:, 2:4, 0:P]
        sg = xt[:, 0:2, P:P + I1]
        z = xt[:, 2:4, P:P + I1]
        zT = yT[:, :, :].rearrange("p (b c) t -> p b c t", b=2)
        y_sb = x1[:, 0:2, :]
        xc = x1[:, 2:4, :]
        gath = stage[:, :, :, :]

        Y, X1T, HT, H, R0, R1, Q, QT = bank
        RB = (R0, R1)
        rank_ps = X1T[:, 0:2 * E1]
        s_ps = QT[:, P:P + E1]
        b_qs, b_gu, b_zT, b_y = Y, (X1T, HT), H, (Q, QT)

        def back(u, p, lag, n):
            d = p - lag
            return u + d // n, d % n

        def live(u, p, n, count):
            return not isinstance(u, int) or 0 <= n * u + p < count

        def late(u, p, n, k):
            return not isinstance(u, int) or n * u + p >= k

        def passes(eng, n, count, lag, lead, body):
            first = -(-(lag + n) // n)
            last = (count - lead) // n
            for i in range(-lead, first * n):
                body(i // n, i % n)
            with eng.Fori(first, last) as u:
                for p in range(n):
                    body(u, p)
            for i in range(last * n, count + lag):
                body(i // n, i % n)

        block = ctx.enter_context(nc.Block())

        @block.sync
        def _(sp):
            for dst, src in ((gl0_sb[:, :, :], gate_lora0), (base_w_sb[:, :, :], base_w),
                             (lb0_sb[:, :], lora_b0), (ab_sb[:, :, :], adapter_b),
                             (aa_sb[:, :, :], adapter_a), (g1_sb[:, :, :], gate1)):
                sp.dma_start(dst, src).then_inc(s["weights0"], 16)
            for b in range(2):
                sp.dma_start(stage[:, b, :, :], gate_up[b]).then_inc(st_in[b], 16)
            sp.dma_start(wd_all[:, :, :, :], down).then_inc(s["wd_loaded"], 16)

            def step(u, p):
                if live(u, p, U, NT):
                    if late(u, p, U, U):
                        sp.wait_ge(s["yT_mm"], U * u + p - U + 1)
                        sp.wait_ge(s["xb_ready"], U * u + p - U + 1)
                    sp.dma_start(xt[:, p, :], xr[bass.ts(U * u + p, P), :]).then_inc(x_in[p], 16)
                v, w = back(u, p, 6, U)
                if live(v, w, U, NT):
                    sp.wait_ge(s["x1_ready"], U * v + w + 1)
                    sp.dma_start(x1_dram[bass.ts(U * v + w, P), :], x1[:, w, :]).then_inc(x1_out[w], 16)

            passes(sp, U, NT, 6, 0, step)

            def load_stage(u, b):
                sp.wait_ge(s["m_mm"], 2 * u + b - 1)
                sp.dma_start(stage[:, b, :, :], gate_up[2 * u + b]).then_inc(st_in[b], 16)

            with sp.Fori(1, NE // 2) as u:
                load_stage(u, 0)
                load_stage(u, 1)
            load_stage(NE // 2, 0)

            sp.wait_ge(s["tables"], 2)
            sp.wait_ge(s["pads"], 16 * E1)
            sp.wait_ge(s["spare_zero"], 16 * SPARE)
            for p in range(U):
                sp.wait_ge(scat[p], 16 * K1 * (NT // U))
                sp.wait_ge(x1_out[p], 16 * (NT // U))

            def tile_step(u, p):
                if live(u, p, 2, NS):
                    if late(u, p, 2, 2):
                        sp.wait_ge(s["qs_mm"], 2 * u + p - 1)
                    row = sp.value_load(tile_row[0:1, bass.ds(2 * u + p, 1)], min_val=0, max_val=ROWS - P)
                    sp.dma_start(qs[:, p, :], q_rows[bass.ds(row, P), :]).then_inc(qs_in[p], 16)
                v, w = back(u, p, 4, 2)
                if live(v, w, 2, NS):
                    sp.wait_ge(s["y_sb"], 2 * v + w + 1)
                    sp.dma_start(y_rows[bass.ts(2 * v + w, P), :], y_sb[:, w, :]).then_inc(y_out[w], 16)

            passes(sp, 2, NS, 4, 0, tile_step)

            def last_step(u, p):
                if live(u, p, 2, NT):
                    if late(u, p, 2, 2):
                        sp.wait_ge(o_out[p], 16 * u)
                    sp.dma_start(xc[:, p, :], x1_dram[bass.ts(2 * u + p, P), :]).then_inc(xc_in[p], 16)
                v, w = back(u, p, 1, 2)
                if live(v, w, 2, NT):
                    sp.wait_ge(s["out_ready"], 2 * v + w + 1)
                    sp.dma_start(outr[bass.ts(2 * v + w, P), :], xc[:, w, :]).then_inc(o_out[w], 16)

            passes(sp, 2, NT, 1, 0, last_step)
            for p in range(2):
                sp.wait_ge(o_out[p], 16 * (NT // 2))

        @block.gpsimd
        def _(pool):
            pool.memset(ident[:, :], 0.0).then_inc(s["ident0"], 1)
            pool.memset(ones[:, :], 1.0).then_inc(s["ident0"], 1)
            pool.memset(zero_rows[:, :], 0.0).then_inc(s["ident0"], 1)
            pool.iota(part_i[:, :], pattern=[[0, 1]], base=0, channel_multiplier=1).then_inc(s["ident0"], 1)
            pool.iota(iota_e[:, :], pattern=[[1, E1]], base=0, channel_multiplier=0,
                      allow_small_or_imprecise_dtypes=True).then_inc(s["ident0"], 1)
            pool.iota(iota_a[:, :, :], pattern=[[1, NA], [0, R]], base=0, channel_multiplier=0,
                      allow_small_or_imprecise_dtypes=True).then_inc(s["ident0"], 1)
            pool.iota(region_f[:, :], pattern=[[REGION, E1]], base=0, channel_multiplier=0,
                      allow_small_or_imprecise_dtypes=True).then_inc(s["ident0"], 1)
            pool.iota(iota_s[:, :], pattern=[[1, NS]], base=0, channel_multiplier=0,
                      allow_small_or_imprecise_dtypes=True).then_inc(s["ident0"], 1)
            pool.wait_ge(s["ident0"], 8)
            pool.affine_select(out=ident[:, :], in_=ident[:, :], compare_op=ALU.not_equal, fill=1.0, base=0,
                               pattern=[[-1, P]], channel_multiplier=1).then_inc(s["consts"], 1)
            pool.affine_select(out=tri[:, :], in_=ones[:, :], compare_op=ALU.is_gt, fill=0.0, base=0,
                               pattern=[[1, P]], channel_multiplier=-1).then_inc(s["consts"], 1)
            pool.affine_select(out=diag[:, :, :], in_=ones[:, :].rearrange("p (b d) -> p b d", b=BPT),
                               compare_op=ALU.is_ge, fill=0.0, base=0, pattern=[[-SEQ, BPT], [0, SEQ]],
                               channel_multiplier=1).then_inc(s["consts"], 1)
            pool.wait_ge(s["consts"], 3)
            pool.affine_select(out=diag[:, :, :], in_=diag[:, :, :], compare_op=ALU.is_ge, fill=0.0,
                               base=SEQ - 1, pattern=[[SEQ, BPT], [0, SEQ]],
                               channel_multiplier=-1).then_inc(s["consts"], 1)
            pool.wait_ge(s["consts"], 4)
            pool.wait_ge(s["cond_row"], 1)
            for n in range(SPARE):
                pool.dma_start(q_rows[E1 * REGION + n * P:E1 * REGION + (n + 1) * P, :],
                               zero_rows[:, :]).then_inc(s["spare_zero"], 16)

            def step(u, p):
                v, w = back(u, p, -1, U)
                if live(v, w, U, NT):
                    if late(v, w, U, U):
                        pool.wait_ge(s["bd_ready"], U * v + w - U + 1)
                    pool.tensor_copy(cidx[:, w:w + 1], cond_row[:, bass.ds(U * v + w, 1)])\
                        .then_inc(s["ci_ready"], 1)
                    pool.wait_ge(s["ci_ready"], U * v + w + 1)
                    pool.sem_inc(s["pool_held"])
                    pool.indirect_dma_start(
                        out=wrow[:, w, :], out_offset=None, in_=cond_w,
                        in_offset=bass.IndirectOffsetOnAxis(ap=cidx[:, w:w + 1], axis=0)).then_inc(w_in[w], 16)
                if live(u, p, U, NT):
                    t = U * u + p
                    pool.wait_ge(w_in[p], 16 * u + 16)
                    if late(u, p, U, 2):
                        pool.wait_ge(s["yT_mm"], t - 1)
                    pool.tensor_tensor(bd[:, p % 2, :, :], wrow[:, p:p + 1, :].broadcast_to([P, BPT, SEQ]),
                                       diag[:, :, :], ALU.mult).then_inc(s["bd_ready"], 1)
                    pool.wait_ge(x_in[p], 16 * u + 16)
                    if late(u, p, U, 2):
                        pool.wait_ge(s["x1_ready"], t - 1)
                    pool.tensor_tensor(xb[:, p % 2, :], xt[:, p, :], base_b_sb[:, :], ALU.add)\
                        .then_inc(s["xb_ready"], 1)
                v, w = back(u, p, 5, U)
                if live(v, w, U, NT):
                    pool.wait_ge(s["slots_ready"], U * v + w + 1)
                    pool.sem_inc(s["pool_held"])
                    for k in range(K1):
                        pool.indirect_dma_start(
                            out=q_rows, out_offset=bass.IndirectOffsetOnAxis(ap=slot_i[:, w, k:k + 1], axis=0),
                            in_=q_sb[:, w, :, :].rearrange("p a r -> p (a r)"), in_offset=None)\
                            .then_inc(scat[w], 16)

            passes(pool, U, NT, 5, 1, step)
            pool.wait_ge(s["pad_ready"], 1)
            for e in range(E1):
                pool.indirect_dma_start(
                    out=q_rows, out_offset=bass.IndirectOffsetOnAxis(ap=pad_i[:, e:e + 1], axis=0),
                    in_=zero_rows[:, :], in_offset=None).then_inc(s["pads"], 16)
            for p in range(2):
                pool.wait_ge(y_out[p], 16 * (NS // 2))

            def gather_step(u, p):
                pool.wait_ge(s["gi_ready"], 2 * u + p + 1)
                pool.sem_inc(s["pool_held"])
                for k in range(K1):
                    pool.indirect_dma_start(
                        out=gath[:, p, k, :], out_offset=None, in_=y_rows,
                        in_offset=bass.IndirectOffsetOnAxis(ap=slot_i[:, p, k:k + 1], axis=0))\
                        .then_inc(g_in[p], 16)

            passes(pool, 2, NT, 0, 0, gather_step)

        @block.scalar
        def _(act):
            for b in range(BPT):
                act.dma_start(cond_i[b * SEQ:(b + 1) * SEQ, :],
                              cond[b:b + 1, :].broadcast_to([SEQ, NT]))\
                    .then_inc(s["idx0"], 1 * 16)
                act.dma_start(adapter_i[b * SEQ:(b + 1) * SEQ, :],
                              adapters[b:b + 1, :].broadcast_to([SEQ, NT]))\
                    .then_inc(s["idx0"], 1 * 16)
            act.dma_start(base_b_sb[:, :], base_b.rearrange("(a d) -> a d", a=1).broadcast_to([P, D]))\
                .then_inc(s["idx0"], 16)
            act.dma_start(bias_sb[:, :], bias1.rearrange("(a d) -> a d", a=1).broadcast_to([P, E1]))\
                .then_inc(s["idx0"], 16)
            act.wait_ge(s["gate_q_mm"], 1)
            act.copy(gate_q[:, :], Q[:, 0:E1]).then_inc(s["gate_q_ready"], 1)

            def step(u, p):
                if live(u, p, U, NT):
                    t = U * u + p
                    act.wait_ge(s["yT_mm"], t + 1)
                    if late(u, p, U, 1):
                        act.wait_ge(s["r_mm"], t)
                    act.copy(yT[:, :, :].rearrange("p c t -> p (c t)"), Y[:, :]).then_inc(s["yT_ready"], 1)
                v, w = back(u, p, 2, U)
                if live(v, w, U, NT):
                    t = U * v + w
                    act.wait_ge(s["x1T_mm"], t + 1)
                    if late(v, w, U, 1):
                        act.wait_ge(s["q_mm"], t)
                    act.copy(x1T[:, :, :].rearrange("p c t -> p (c t)"), X1T[:, :]).then_inc(s["x1T_ready"], 1)
                v, w = back(u, p, 1, U)
                if live(v, w, U, NT):
                    t = U * v + w
                    act.wait_ge(s["hwT_mm"], t + 1)
                    act.copy(hwT[:, :], HT[:, 0:P]).then_inc(s["hwT_ready"], 1)
                if live(u, p, U, NT):
                    t = U * u + p
                    act.wait_ge(s["d_ready"], t + 1)
                    act.activation(r0[:, 16:24], r0[:, 8:16], ACT.Exp, accum_out=r0[:, 24:25])\
                        .then_inc(s["exp0"], 1)
                v, w = back(u, p, 2, U)
                if live(v, w, U, NT):
                    t = U * v + w
                    act.wait_ge(s["qT_mm"], t + 1)
                    if late(v, w, U, 1):
                        act.wait_ge(s["s_mm"], t)
                    act.copy(qT[:, :], QT[:, 0:P]).then_inc(s["qT_ready"], 1)
                    act.copy(qT_all[:, bass.ds(t, 1), :].rearrange("p a t -> p (a t)"), QT[:, 0:P])\
                        .then_inc(s["qT_ready"], 1)
                    act.wait_ge(s["s_mm"], t + 1)
                    if late(v, w, U, 1):
                        act.wait_ge(s["mask_ready"], t)
                    act.activation(r1[:, 0:16], s_ps, ACT.Exp, scale=-1.0).then_inc(s["exp1"], 1)

            passes(act, U, NT, 2, 0, step)

            def fold(u, b):
                e = 2 * u + b
                act.wait_ge(s["m_mm"], e + 1)
                act.copy(m_all[:, bass.ds(e, 1), :].rearrange("p a n -> p (a n)"), RB[b][:, :])\
                    .then_inc(s["m_ready"], 1)

            with act.Fori(0, NE // 2) as u:
                fold(u, 0)
                fold(u, 1)
            fold(NE // 2, 0)

            def tile_step(u, p):
                if live(u, p, 2, NS):
                    i = 2 * u + p
                    act.wait_ge(s["qs_mm"], i + 1)
                    if late(u, p, 2, 2):
                        act.wait_ge(s["gu_mm"], i - 1)
                    act.copy(qsT[:, p, :], b_qs[:, 0:P]).then_inc(s["qs_ready"], 1)
                v, w = back(u, p, 1, 2)
                if live(v, w, 2, NS):
                    i = 2 * v + w
                    act.wait_ge(s["zT_mm"], i + 1)
                    if late(v, w, 2, 2):
                        act.wait_ge(s["y_mm"], i - 1)
                    act.copy(zT[:, w, :, :].rearrange("p c t -> p (c t)"), b_zT[:, 0:I1]).then_inc(s["zT_ready"], 1)
                if live(u, p, 2, NS):
                    i = 2 * u + p
                    act.wait_ge(s["gu_mm"], i + 1)
                    if late(u, p, 2, 2):
                        act.wait_ge(s["z_ready"], i - 1)
                    act.activation(sg[:, p, :], b_gu[p][:, 0:I1], ACT.Silu).then_inc(s["silu_done"], 1)

            passes(act, 2, NS, 1, 0, tile_step)

            def last_step(u, p):
                if live(u, p, 2, NT):
                    i = NS + 2 * u + p
                    act.wait_ge(s["gu_mm"], i - 1)
                    act.copy(qsT[:, p, :], qT_all[:, bass.ds(2 * u + p, 1), :].rearrange("p a t -> p (a t)"))\
                        .then_inc(s["qs_ready"], 1)
                v, w = back(u, p, 1, 2)
                if live(v, w, 2, NT):
                    i = NS + 2 * v + w
                    act.wait_ge(s["zT_mm"], i + 1)
                    act.wait_ge(s["y_mm"], i - 1)
                    act.copy(zT[:, w, :, :].rearrange("p c t -> p (c t)"), b_zT[:, 0:I1]).then_inc(s["zT_ready"], 1)
                if live(u, p, 2, NT):
                    i = NS + 2 * u + p
                    act.wait_ge(s["gu_mm"], i + 1)
                    act.wait_ge(s["z_ready"], i - 1)
                    act.activation(sg[:, p, :], b_gu[p][:, 0:I1], ACT.Silu).then_inc(s["silu_done"], 1)

            passes(act, 2, NT, 1, 0, last_step)

        @block.tensor
        def _(pe):
            def mm(o, lhsT, rhs, start, stop):
                return pe.matmul(o, lhsT, rhs, start=start, stop=stop)

            pe.wait_ge(s["consts"], 4)
            pe.wait_ge(s["weights0"], 16 * 6)
            for c in range(KC):
                last = mm(Q[:, 0:E1], aa_sb[:, c, :], g1_sb[:, c, :], c == 0, c == KC - 1)
            last.then_inc(s["gate_q_mm"], 1)
            pe.wait_ge(s["gate_q_ready"], 1)

            def step(u, p):
                if live(u, p, U, NT):
                    t = U * u + p
                    pe.wait_ge(x_in[p], 16 * u + 16)
                    pe.wait_ge(s["bd_ready"], t + 1)
                    if late(u, p, U, 1):
                        pe.wait_ge(s["yT_ready"], t)
                    for c in range(KC):
                        last = mm(Y[:, c * P:(c + 1) * P], xt[:, p, c * P:(c + 1) * P],
                                  bd[:, p % 2, :, :].rearrange("p b d -> p (b d)"), True, True)
                    last.then_inc(s["yT_mm"], 1)
                v, w = back(u, p, 2, U)
                if live(v, w, U, NT):
                    t = U * v + w
                    pe.wait_ge(s["x1_ready"], t + 1)
                    if late(v, w, U, 1):
                        pe.wait_ge(s["x1T_ready"], t)
                    v4, w4 = back(v, w, 2, U)
                    if live(v4, w4, U, NT):
                        pe.wait_ge(s["rank_done"], t - 1)
                    for c in range(KC):
                        last = pe.transpose(X1T[:, c * P:(c + 1) * P], x1[:, w, c * P:(c + 1) * P], ident[:, :])
                    last.then_inc(s["x1T_mm"], 1)
                v, w = back(u, p, 1, U)
                if live(v, w, U, NT):
                    t = U * v + w
                    pe.wait_ge(s["hw_ready"], t + 1)
                    if late(v, w, U, 1):
                        pe.wait_ge(s["hwT_ready"], t)
                    pe.transpose(HT[:, 0:P], hw[:, :, :].rearrange("p e r -> p (e r)"), ident[:, :])\
                        .then_inc(s["hwT_mm"], 1)
                if live(u, p, U, NT):
                    t = U * u + p
                    pe.wait_ge(s["yT_ready"], t + 1)
                    if late(u, p, U, 1):
                        pe.wait_ge(s["hw_ready"], t)
                    for c in range(KC):
                        last = mm(H[:, 0:E0 + E0 * R], yT[:, c, :], gl0_sb[:, c, :], c == 0, c == KC - 1)
                    last.then_inc(s["h_mm"], 1)
                v, w = back(u, p, 2, U)
                if live(v, w, U, NT):
                    t = U * v + w
                    pe.wait_ge(s["x1T_ready"], t + 1)
                    if late(v, w, U, 1):
                        pe.wait_ge(s["q_ready"], t)
                    for c in range(KC):
                        last = mm(Q[:, 0:P], x1T[:, c, :], ab_sb[:, c, :], c == 0, c == KC - 1)
                    last.then_inc(s["q_mm"], 1)
                if live(u, p, U, NT):
                    t = U * u + p
                    if late(u, p, U, 2):
                        pe.wait_ge(s["x1_ready"], t - 1)
                    for c in range(KC):
                        last = mm(RB[p % 2][:, :], yT[:, c, :], base_w_sb[:, c, :], c == 0, False)
                    last.then_inc(s["r_mm"], 1)
                v, w = back(u, p, 2, U)
                if live(v, w, U, NT):
                    t = U * v + w
                    pe.wait_ge(s["q_ready"], t + 1)
                    if late(v, w, U, 1):
                        pe.wait_ge(s["exp1"], t)
                    pe.transpose(QT[:, 0:P], q_sb[:, w, :, :].rearrange("p a r -> p (a r)"), ident[:, :])\
                        .then_inc(s["qT_mm"], 1)
                v, w = back(u, p, 1, U)
                if live(v, w, U, NT):
                    t = U * v + w
                    pe.wait_ge(s["hwT_ready"], t + 1)
                    mm(RB[w % 2][:, :], hwT[:, :], lb0_sb[:, :], False, True).then_inc(s["g1mm"], 1)
                v, w = back(u, p, 2, U)
                if live(v, w, U, NT):
                    t = U * v + w
                    pe.wait_ge(s["qT_ready"], 2 * t + 2)
                    mm(s_ps, qT[:, :], gate_q[:, :], True, True).then_inc(s["s_mm"], 1)
                v, w = back(u, p, 3, U)
                if live(v, w, U, NT):
                    t = U * v + w
                    pe.wait_ge(s["mask_ready"], t + 1)
                    if not isinstance(u, int) or U * u + p - 2 < NT:
                        pe.wait_ge(s["x1T_ready"], t + 2)
                    if late(v, w, U, 1):
                        pe.wait_ge(s["rank_done"], t)
                    mm(rank_ps[:, 0:E1], tri[:, :], mask[:, w % 2, :], True, True)
                    mm(rank_ps[:, E1:2 * E1], ones[:, :], mask[:, w % 2, :], True, True).then_inc(s["rank_mm"], 1)

            passes(pe, U, NT, 3, 0, step)

            pe.wait_ge(s["x1_ready"], NT)

            def fold(u, b, first):
                e = 2 * u + b
                if not first:
                    pe.wait_ge(s["m_ready"], e - 1)
                pe.wait_ge(st_in[b], 16 * u + 16)
                for c in range(KC):
                    last = mm(RB[b][:, :], aa_sb[:, c, :], stage[:, b, c, :], c == 0, c == KC - 1)
                last.then_inc(s["m_mm"], 1)

            fold(0, 0, True)
            fold(0, 1, True)
            with pe.Fori(1, NE // 2) as u:
                fold(u, 0, False)
                fold(u, 1, False)
            fold(NE // 2, 0, False)

            pe.wait_ge(s["m_ready"], NE)
            pe.wait_ge(s["wd_loaded"], 16)
            pe.wait_ge(s["tables"], 2)
            pe.wait_ge(s["rank_done"], NT)
            pe.wait_ge(s["exp1"], NT)

            def down_product(i, w, e):
                pe.wait_ge(s["zT_ready"], i + 1)
                for c in range(IC):
                    rhs = wd_all[:, e, c, :] if isinstance(e, int) else \
                        wd_all[:, bass.ds(e, 1), c, :].rearrange("p a n -> p (a n)")
                    last = mm(b_y[w][:, :], zT[:, w, c, :], rhs, c == 0, c == IC - 1)
                last.then_inc(s["y_mm"], 1)

            def turn_z(i, w, first):
                pe.wait_ge(s["z_ready"], i + 1)
                if not first:
                    pe.wait_ge(s["zT_ready"], i)
                for c in range(IC):
                    last = pe.transpose(b_zT[:, c * P:(c + 1) * P], z[:, w, c * P:(c + 1) * P], ident[:, :])
                last.then_inc(s["zT_mm"], 1)

            def gate_up_product(i, p, e):
                pe.wait_ge(s["qs_ready"], i + 1)
                rhs = m_all[:, e, :] if isinstance(e, int) else \
                    m_all[:, bass.ds(e, 1), :].rearrange("p a n -> p (a n)")
                mm(b_gu[p][:, :], qsT[:, p, :], rhs, True, True).then_inc(s["gu_mm"], 1)

            def expert_of(i):
                return pe.value_load(tile_e[0:1, bass.ds(i, 1)], min_val=0, max_val=NE - 1)

            def tile_step(u, p):
                if live(u, p, 2, NS):
                    i = 2 * u + p
                    pe.wait_ge(qs_in[p], 16 * u + 16)
                    if late(u, p, 2, 1):
                        pe.wait_ge(s["qs_ready"], i)
                    pe.transpose(b_qs[:, 0:P], qs[:, p, :], ident[:, :]).then_inc(s["qs_mm"], 1)
                v, w = back(u, p, 2, 2)
                if live(v, w, 2, NS):
                    i = 2 * v + w
                    if late(v, w, 2, 2):
                        pe.wait_ge(s["y_sb"], i - 1)
                    down_product(i, w, expert_of(i))
                v, w = back(u, p, 1, 2)
                if live(v, w, 2, NS):
                    turn_z(2 * v + w, w, not late(v, w, 2, 1))
                if live(u, p, 2, NS):
                    i = 2 * u + p
                    if late(u, p, 2, 2):
                        pe.wait_ge(s["z_ready"], i - 1)
                    gate_up_product(i, p, expert_of(i))

            passes(pe, 2, NS, 2, 0, tile_step)

            def last_step(u, p):
                v, w = back(u, p, 2, 2)
                if live(v, w, 2, NT):
                    i = NS + 2 * v + w
                    if late(v, w, 2, 2):
                        pe.wait_ge(s["sh_y"], 2 * v + w - 1)
                    else:
                        pe.wait_ge(s["y_sb"], i - 1)
                    down_product(i, w, NE - 1)
                v, w = back(u, p, 1, 2)
                if live(v, w, 2, NT):
                    turn_z(NS + 2 * v + w, w, False)
                if live(u, p, 2, NT):
                    i = NS + 2 * u + p
                    pe.wait_ge(s["z_ready"], i - 1)
                    gate_up_product(i, p, NE - 1)

            passes(pe, 2, NT, 2, 0, last_step)

        @block.vector
        def _(dve):
            dve.wait_ge(s["ident0"], 8)
            dve.wait_ge(s["idx0"], 16 * (2 * BPT + 2))
            dve.tensor_scalar(c_i[:, :], part_i[:, :], SEQ - 1, None, ALU.bitwise_and).then_inc(s["t_step"], 1)
            dve.wait_ge(s["t_step"], 1)
            dve.tensor_copy(c_f[:, :], c_i[:, :]).then_inc(s["t_step"], 1)
            dve.tensor_copy(part_f[:, :], part_i[:, :]).then_inc(s["t_step"], 1)
            dve.tensor_copy(adapter_f[:, :], adapter_i[:, :]).then_inc(s["t_step"], 1)
            dve.tensor_copy(rowno[:, :], region_f[:, :]).then_inc(s["t_step"], 1)
            dve.wait_ge(s["t_step"], 5)
            dve.tensor_scalar(cond_row[:, :], cond_i[:, :], float(SEQ), c_f[:, 0:1], ALU.mult, ALU.add)\
                .then_inc(s["cond_row"], 1)

            def ranks(u, p):
                t = U * u + p
                at = t * 4

                dve.wait_ge(s["rank_mm"], t + 1)
                dve.tensor_tensor(rk[:, :], rank_ps[:, 0:E1], rowno[:, :], ALU.add).then_inc(s["rank_step"], 1)
                dve.wait_ge(s["rank_step"], at + 1)
                dve.tensor_tensor(ohr[:, :, :], oh[:, :, :],
                                  rk[:, :].rearrange("p (a e) -> p a e", a=1).broadcast_to([P, K1, E1]), ALU.mult)\
                    .then_inc(s["rank_step"], 1)
                dve.tensor_tensor(rowno[:, :], rowno[:, :], rank_ps[:, E1:2 * E1], ALU.add)\
                    .then_inc(s["rank_done"], 1)
                dve.wait_ge(s["rank_step"], at + 2)
                dve.tensor_reduce(slot_f[:, :], ohr[:, :, :], AX.X, ALU.add).then_inc(s["rank_step"], 1)
                if late(u, p, U, U):
                    dve.wait_ge(scat[p], 16 * K1 * u)
                dve.wait_ge(s["rank_step"], at + 3)
                dve.tensor_copy(slot_i[:, p, :], slot_f[:, :]).then_inc(s["slots_ready"], 1)
                dve.tensor_copy(slots[:, bass.ds(t, 1), :].rearrange("p a k -> p (a k)"), slot_f[:, :])\
                    .then_inc(s["rank_step"], 1)

            def route1(u, p):
                t = U * u + p
                n = [t * 10]

                def link(ins):
                    ins.then_inc(s["r1_step"], 1)
                    n[0] = n[0] + 1
                    dve.wait_ge(s["r1_step"], n[0])

                dve.wait_ge(s["exp1"], t + 1)
                link(dve.tensor_scalar(r1[:, 16:32], r1[:, 0:16], 1.0, None, ALU.add))
                link(dve.reciprocal(r1[:, 32:48], r1[:, 16:32]))
                link(dve.tensor_tensor(r1[:, 48:64], r1[:, 32:48], bias_sb[:, :], ALU.add))
                dve.sem_inc(s["dve_held"])
                link(dve.max(r1[:, 64:72], r1[:, 48:64]))
                dve.sem_inc(s["dve_held"])
                link(dve.max_index(r1i[:, :], r1[:, 64:72], r1[:, 48:64]))
                link(dve.tensor_copy(r1[:, 72:76], r1i[:, 0:K1]))
                dve.tensor_copy(chosen[:, bass.ds(t, 1), :].rearrange("p a k -> p (a k)"), r1i[:, 0:K1])
                link(dve.tensor_reduce(r1[:, 76:77], r1[:, 64:68], AX.X, ALU.add))
                link(dve.tensor_scalar(r1[:, 77:78], r1[:, 76:77], 1e-20, None, ALU.add))
                link(dve.reciprocal(r1[:, 78:79], r1[:, 77:78]))
                dve.tensor_scalar(w_all[:, bass.ds(t, 1), :].rearrange("p a k -> p (a k)"), r1[:, 64:68],
                                  r1[:, 78:79], None, ALU.mult)
                if late(u, p, U, 1):
                    dve.wait_ge(s["rank_step"], t * 4)
                link(dve.tensor_tensor(
                    oh[:, :, :], iota_e[:, :].rearrange("p (a e) -> p a e", a=1).broadcast_to([P, K1, E1]),
                    r1[:, 72:76].rearrange("p (k a) -> p k a", a=1).broadcast_to([P, K1, E1]), ALU.is_equal))
                dve.tensor_reduce(mask[:, p % 2, :], oh[:, :, :].rearrange("p k e -> p e k"), AX.X, ALU.add)\
                    .then_inc(s["mask_ready"], 1)

            def route0(u, p):
                t = U * u + p
                n = [t * 10]

                def link(ins):
                    ins.then_inc(s["r0_step"], 1)
                    n[0] = n[0] + 1
                    dve.wait_ge(s["r0_step"], n[0])

                dve.wait_ge(s["h_mm"], t + 1)
                dve.sem_inc(s["dve_held"])
                link(dve.max(r0[:, 0:8], H[:, 0:E0]))
                dve.tensor_scalar(r0[:, 8:16], H[:, 0:E0], r0[:, 0:1], None, ALU.subtract)\
                    .then_inc(s["d_ready"], 1)
                dve.wait_ge(s["exp0"], t + 1)
                link(dve.reciprocal(r0[:, 25:26], r0[:, 24:25]))
                link(dve.tensor_scalar(r0[:, 32:40], r0[:, 16:24], r0[:, 25:26], None, ALU.mult))
                dve.sem_inc(s["dve_held"])
                link(dve.max(r0[:, 40:48], r0[:, 32:40]))
                dve.sem_inc(s["dve_held"])
                link(dve.max_index(r0i[:, :], r0[:, 40:48], r0[:, 32:40]))
                link(dve.tensor_tensor(r0[:, 48:49], r0[:, 40:41], r0[:, 41:42], ALU.add))
                link(dve.reciprocal(r0[:, 49:50], r0[:, 48:49]))
                dve.tensor_copy(r0[:, 52:54], r0i[:, 0:K0])
                link(dve.tensor_scalar(r0[:, 50:52], r0[:, 40:42], r0[:, 49:50], None, ALU.mult))
                dve.tensor_scalar(r0[:, 56:64], iota_e[:, 0:E0], r0[:, 52:53], r0[:, 50:51], ALU.is_equal, ALU.mult)
                link(dve.tensor_scalar(r0[:, 64:72], iota_e[:, 0:E0], r0[:, 53:54], r0[:, 51:52],
                                       ALU.is_equal, ALU.mult))
                link(dve.tensor_tensor(r0[:, 72:80], r0[:, 56:64], r0[:, 64:72], ALU.add))
                if late(u, p, U, 1):
                    dve.wait_ge(s["hwT_mm"], t)
                dve.tensor_tensor(hw[:, :, :], H[:, E0:E0 + E0 * R].rearrange("p (e r) -> p e r", e=E0),
                                  r0[:, 72:80].rearrange("p (e a) -> p e a", a=1).broadcast_to([P, E0, R]),
                                  ALU.mult).then_inc(s["hw_ready"], 1)

            def step(u, p):
                v, w = back(u, p, 4, U)
                if live(v, w, U, NT):
                    ranks(v, w)
                v, w = back(u, p, 2, U)
                if live(v, w, U, NT):
                    t = U * v + w
                    dve.wait_ge(s["g1mm"], t + 1)
                    dve.wait_ge(s["xb_ready"], t + 1)
                    if late(v, w, U, 4):
                        dve.wait_ge(x1_out[w], 16 * v)
                    dve.tensor_tensor(x1[:, w, :], RB[w % 2][:, :], xb[:, w % 2, :], ALU.add)\
                        .then_inc(s["x1_ready"], 1)
                v, w = back(u, p, 3, U)
                if live(v, w, U, NT):
                    route1(v, w)
                v, w = back(u, p, 2, U)
                if live(v, w, U, NT):
                    t = U * v + w
                    dve.wait_ge(s["q_mm"], t + 1)
                    if late(v, w, U, U):
                        dve.wait_ge(scat[w], 16 * K1 * v)
                    dve.scalar_tensor_tensor(
                        out=q_sb[:, w, :, :].rearrange("p a r -> p (a r)"),
                        in0=iota_a[:, :, :].rearrange("p a r -> p (a r)"), scalar=adapter_f[:, bass.ds(t, 1)],
                        in1=Q[:, 0:P], op0=ALU.is_equal, op1=ALU.mult).then_inc(s["q_ready"], 1)
                if live(u, p, U, NT):
                    route0(u, p)

            passes(dve, U, NT, 4, 0, step)

            n = [5]

            def link(ins):
                ins.then_inc(s["t_step"], 1)
                n[0] += 1
                dve.wait_ge(s["t_step"], n[0])

            dve.wait_ge(s["rank_done"], NT)
            dve.tensor_scalar(pad_i[:, :], rowno[:, :], part_f[:, 0:1], None, ALU.add).then_inc(s["pad_ready"], 1)
            link(dve.tensor_tensor(tf[:, 0, :], rowno[:, :], region_f[:, :], ALU.subtract))
            link(dve.tensor_scalar(ti[:, 0, :], tf[:, 0, :], float(P - 1), None, ALU.add))
            link(dve.tensor_scalar(ti[:, 1, :], ti[:, 0, :], P.bit_length() - 1, None, ALU.arith_shift_right))
            link(dve.tensor_copy(tf[:, 1, :], ti[:, 1, :]))
            link(dve.tensor_copy(tf[:, 2, :], tf[:, 1, :]))
            a, b = 2, 3
            d = 1
            while d < E1:
                dve.tensor_copy(tf[:, b, 0:d], tf[:, a, 0:d])
                link(dve.tensor_tensor(tf[:, b, d:E1], tf[:, a, d:E1], tf[:, a, 0:E1 - d], ALU.add))
                a, b = b, a
                d *= 2
            one = slice(0, 1)
            link(dve.tensor_tensor(
                ge[one, :, :], iota_s[one, :].rearrange("p (s a) -> p s a", a=1).broadcast_to([1, NS, E1]),
                tf[one, a, :].rearrange("p (a e) -> p a e", a=1).broadcast_to([1, NS, E1]), ALU.is_ge))
            link(dve.tensor_reduce(ts[one, 0, :], ge[one, :, :], AX.X, ALU.add))
            link(dve.tensor_tensor(
                ge[one, :, :], ge[one, :, :],
                tf[one, 1, :].rearrange("p (a e) -> p a e", a=1).broadcast_to([1, NS, E1]), ALU.mult))
            link(dve.tensor_reduce(ts[one, 1, :], ge[one, :, :], AX.X, ALU.add))
            link(dve.tensor_tensor(ts[one, 2, :], iota_s[one, :], ts[one, 1, :], ALU.subtract))
            link(dve.tensor_scalar(ts[one, 2, :], ts[one, 2, :], float(P), None, ALU.mult))
            link(dve.tensor_scalar(ts[one, 3, :], ts[one, 0, :], float(REGION), None, ALU.mult))
            dve.tensor_tensor(tile_row[:, :], ts[one, 3, :], ts[one, 2, :], ALU.add).then_inc(s["tables"], 1)
            dve.tensor_copy(tile_e[:, :], ts[one, 0, :]).then_inc(s["tables"], 1)
            link(dve.tensor_tensor(tf[:, 4, :], tf[:, a, :], tf[:, 1, :], ALU.subtract))
            link(dve.scalar_tensor_tensor(out=tf[:, 5, :], in0=tf[:, 4, :], scalar=float(P), in1=region_f[:, :],
                                          op0=ALU.mult, op1=ALU.subtract))
            for k in range(K1):
                moved = ge[:, 0:NT, :]
                link(dve.tensor_tensor(
                    moved, iota_e[:, :].rearrange("p (a e) -> p a e", a=1).broadcast_to([P, NT, E1]),
                    chosen[:, :, k:k + 1].broadcast_to([P, NT, E1]), ALU.is_equal))
                link(dve.tensor_tensor(
                    moved, moved, tf[:, 5:6, :].broadcast_to([P, NT, E1]), ALU.mult))
                link(dve.tensor_reduce(shift[:, :], moved, AX.X, ALU.add))
                link(dve.tensor_tensor(y_slots[:, :, k], slots[:, :, k], shift[:, :], ALU.add))
            for p in range(4):
                dve.wait_ge(x1_out[p], 16 * (NT // 4))

            def product_z(i, p):
                dve.wait_ge(s["silu_done"], i + 1)
                dve.tensor_tensor(z[:, p, :], sg[:, p, :], b_gu[p][:, I1:GU], ALU.mult).then_inc(s["z_ready"], 1)

            def tile_step(u, p):
                v, w = back(u, p, 2, 2)
                if live(v, w, 2, NS):
                    i = 2 * v + w
                    dve.wait_ge(s["y_mm"], i + 1)
                    if late(v, w, 2, 2):
                        dve.wait_ge(y_out[w], 16 * v)
                    dve.tensor_copy(y_sb[:, w, :], b_y[w][:, :]).then_inc(s["y_sb"], 1)
                if live(u, p, 2, NS):
                    i = 2 * u + p
                    if late(u, p, 2, 2):
                        dve.wait_ge(s["zT_mm"], i - 1)
                    product_z(i, p)

            passes(dve, 2, NS, 2, 0, tile_step)

            for p in range(U):
                dve.wait_ge(scat[p], 16 * K1 * (NT // U))

            def combine(u, p):
                t = 2 * u + p
                at = t * K1
                dve.wait_ge(s["y_mm"], NS + t + 1)
                dve.wait_ge(xc_in[p], 16 * u + 16)
                dve.tensor_tensor(xc[:, p, :], xc[:, p, :], b_y[p][:, :], ALU.add).then_inc(s["sh_y"], 1)
                dve.wait_ge(s["sh_y"], t + 1)
                dve.wait_ge(g_in[p], 16 * K1 * u + 16 * K1)
                for k in range(K1):
                    last = dve.scalar_tensor_tensor(
                        out=xc[:, p, :], in0=gath[:, p, k, :],
                        scalar=w_all[:, bass.ds(t, 1), k:k + 1].rearrange("p a k -> p (a k)"),
                        in1=xc[:, p, :], op0=ALU.mult, op1=ALU.add)
                    if k < K1 - 1:
                        last.then_inc(s["acc_step"], 1)
                        dve.wait_ge(s["acc_step"], t * (K1 - 1) + k + 1)
                last.then_inc(s["out_ready"], 1)

            def indices(u, p):
                t = 2 * u + p
                if late(u, p, 2, 2):
                    dve.wait_ge(s["out_ready"], t - 1)
                dve.tensor_copy(slot_i[:, p, :], y_slots[:, bass.ds(t, 1), :].rearrange("p a k -> p (a k)"))\
                    .then_inc(s["gi_ready"], 1)

            def last_step(u, p):
                if live(u, p, 2, NT):
                    dve.wait_ge(s["zT_mm"], NS + 2 * u + p - 1)
                    product_z(NS + 2 * u + p, p)
                v, w = back(u, p, 2, 2)
                if live(v, w, 2, NT):
                    combine(v, w)
                if live(u, p, 2, NT):
                    indices(u, p)

            passes(dve, 2, NT, 2, 0, last_step)


def kernel(x, itok_B_0_15, itok_B_3_7, L0_cond_weights, L0_ffn_W_base, L0_ffn_b_base, L0_ffn_W_gate, L0_ffn_A,
           L0_ffn_B, L1_cond_A, L1_cond_B, L1_ffn_gate_w, L1_ffn_bias, L1_ffn_Wg, L1_ffn_Wu, L1_ffn_Wd,
           L1_ffn_Sg, L1_ffn_Su, L1_ffn_Sd):
    import numpy as np
    import concourse.bacc as bacc
    from concourse.bass_utils import run_bass_kernel_spmd

    def arr(a):
        return np.asarray(a)

    def chunks(wt):
        return wt.reshape(KC, P, -1).transpose(1, 0, 2)

    gate0, a0 = arr(L0_ffn_W_gate), arr(L0_ffn_A).reshape(E0 * R, D)
    wg = np.concatenate([arr(L1_ffn_Wg), arr(L1_ffn_Sg)[None]])
    wu = np.concatenate([arr(L1_ffn_Wu), arr(L1_ffn_Su)[None]])
    gu = np.concatenate([wg, wu], axis=1)
    wd = np.concatenate([arr(L1_ffn_Wd), arr(L1_ffn_Sd)[None]])
    arrays = {
        "x": arr(x),
        "cond": arr(itok_B_0_15).reshape(NT, BPT).T,
        "adapters": arr(itok_B_3_7).reshape(NT, BPT).T,
        "cond_w": arr(L0_cond_weights).reshape(-1, SEQ),
        "base_w": chunks(arr(L0_ffn_W_base).T),
        "base_b": arr(L0_ffn_b_base),
        "gate_lora0": chunks(np.concatenate([gate0, a0]).T),
        "lora_b0": arr(L0_ffn_B).transpose(0, 2, 1).reshape(E0 * R, D),
        "adapter_b": chunks(arr(L1_cond_B).reshape(NA * R, D).T),
        "adapter_a": chunks(arr(L1_cond_A).transpose(1, 0, 2).reshape(D, NA * R)),
        "gate1": chunks(arr(L1_ffn_gate_w).T),
        "bias1": arr(L1_ffn_bias),
        "gate_up": gu.reshape(NE, GU, KC, P).transpose(0, 3, 2, 1),
        "down": wd.transpose(2, 0, 1).reshape(IC, P, NE, D).transpose(1, 2, 0, 3),
    }
    nc = bacc.Bacc("TRN2", target_bir_lowering=False, num_devices=1)
    arrays = {f"in_{n}": np.ascontiguousarray(a) for n, a in arrays.items()}
    args = [nc.dram_tensor(n, a.shape, mybir.dt.from_np(a.dtype), kind="ExternalInput").ap()
            for n, a in arrays.items()]
    args.append(nc.dram_tensor("out_0", (BATCH, SEQ, D), F32, kind="ExternalOutput").ap())
    adaln_ffn_kernel(nc, *args)
    r = run_bass_kernel_spmd(nc, [arrays], core_ids=[0])
    return r.results[0]["out_0"]
```

```python
from contextlib import ExitStack

import concourse.bass as bass
from concourse import mybir

F32 = mybir.dt.float32
F32R = mybir.dt.float32r
I32 = mybir.dt.int32
U32 = mybir.dt.uint32
ALU = mybir.AluOpType
ACT = mybir.ActivationFunctionType
AX = mybir.AxisListType

P = 128
BATCH, SEQ, D = 128, 32, 512
TOK = BATCH * SEQ
NT = TOK // P
BPT = P // SEQ
KC = D // P
E0, K0, R = 8, 2, 16
E1, K1, I1 = 16, 4, 256
IC = I1 // P
NE = E1 + 1
NA = 8
GU = 2 * I1
REGION = TOK + P
SPARE = E1
NS = TOK * K1 // P + SPARE
ROWS = E1 * REGION + SPARE * P
U = 4
V = 8
ROW = R + 4
A_COL, W_COL, T_COL = R, R + 1, R + 2
AHEAD = 5
ACC = 2


def adaln_ffn_kernel(nc, x, cond, adapters, cond_w, base_w, base_b, gate_lora0, lora_b0, adapter_b,
                     adapter_a, gate1, bias1, gate_up, down, out):
    q_rows = nc.dram_tensor("q_rows", [ROWS, ROW], F32).ap()
    t_rows = nc.dram_tensor("t_rows", [TOK, ROW], F32).ap()
    acc = [nc.dram_tensor(f"acc{i}", [TOK + P, D], F32).ap() for i in range(ACC)]
    xr = x.rearrange("b s d -> (b s) d")
    outr = out.rearrange("b s d -> (b s) d")

    with ExitStack() as ctx:
        def sb(name, shape, dt=F32):
            return ctx.enter_context(nc.sbuf_tensor(name, shape, dt))

        def sem(name):
            return ctx.enter_context(nc.semaphore(name))

        bank = [ctx.enter_context(nc.psum_tensor(f"bank{i}", [P, 512], F32)) for i in range(8)]

        ident = sb("ident", [P, P])
        ones = sb("ones", [P, P])
        iota_a = sb("iota_a", [P, NA, R])
        pad_row = sb("pad_row", [P, ROW])
        part_i = sb("part_i", [P, 1], I32)
        tile_e = sb("tile_e", [1, NS], I32)
        tile_row = sb("tile_row", [1, NS], I32)
        m_all = sb("m_all", [P, NE, GU])
        aa_sb = sb("aa_sb", [P, KC, NA * R])
        tf = sb("tf", [P, 6, E1])
        ti = sb("ti", [P, 2, E1], I32)
        pad_i = sb("pad_i", [P, E1], U32)

        first_use = ExitStack()

        def sb1(name, shape, dt=F32):
            return first_use.enter_context(nc.sbuf_tensor(name, shape, dt))

        wd_raw = sb1("wd_raw", [P, NE * IC, D])

        stage = [sb1(f"stage{b}", [P, KC, GU])[:, :, :] for b in range(2)]
        with nc.sbuf_tensor("base_w_hi", [P, KC, D], F32R) as base_w_hi:
            pass
        stage.append(sb1("stage2", [P, KC, GU])[:, :, :])
        zero_tile = sb1("zero_tile", [P, D])
        tri = sb1("tri", [P, P])
        tri_r = sb1("tri_r", [P, P], F32R)
        ones_r = sb1("ones_r", [P, P], F32R)
        diag = sb1("diag", [P, BPT, SEQ])
        iota_e = sb1("iota_e", [P, E1])
        part_f = sb1("part_f", [P, 1])
        region_f = sb1("region_f", [P, E1])
        cond_i = sb1("cond_i", [P, NT], I32)
        cond_row = sb1("cond_row", [P, NT], U32)
        c_i = sb1("c_i", [P, 1], I32)
        c_f = sb1("c_f", [P, 1])
        adapter_i = sb1("adapter_i", [P, NT], I32)
        head = sb1("head", [P, NT, ROW - R])
        base_w_lo = sb1("base_w_lo", [P, KC, D], F32R)
        base_b_sb = sb1("base_b_sb", [P, D])
        gl0_sb = sb1("gl0_sb", [P, KC, E0 + E0 * R])
        lb0_sb = sb1("lb0_sb", [P, D])
        lb0_hi = sb1("lb0_hi", [P, D], F32R)
        lb0_lo = sb1("lb0_lo", [P, D], F32R)
        ab_sb = sb1("ab_sb", [P, KC, NA * R])
        g1_sb = sb1("g1_sb", [P, KC, E1])
        gate_q = sb1("gate_q", [P, E1])
        bias_sb = sb1("bias_sb", [P, E1])

        xt = sb1("xt", [P, U, D])
        cidx = sb1("cidx", [P, U], U32)
        wrow = sb1("wrow", [P, U, SEQ])
        bd = sb1("bd", [P, 2, BPT, SEQ])
        yT = sb1("yT", [P, 2, KC, P])
        yT_hi = sb1("yT_hi", [P, 2, KC, P], F32R)
        yT_lo = sb1("yT_lo", [P, 2, KC, P], F32R)
        hw = sb1("hw", [P, E0, R])
        hwT_hi = sb1("hwT_hi", [P, P], F32R)
        hwT_lo = sb1("hwT_lo", [P, P], F32R)
        x1 = sb1("x1", [P, U, D])
        x1T = sb1("x1T", [P, KC, P])
        q_sb = sb1("q_sb", [P, NA, R])
        q16 = sb1("q16", [P, U, 1, R])
        rows = sb1("rows", [P, U, K1, ROW])
        qT = sb1("qT", [P, P])
        slot_i = sb1("slot_i", [P, U, K1], U32)
        top0 = sb1("top0", [P, 8])
        top0_i = sb1("top0_i", [P, 8], U32)
        d0 = sb1("d0", [P, K0])
        exp0 = sb1("exp0", [P, K0])
        sum0 = sb1("sum0", [P, 2])
        oh0 = sb1("oh0", [P, K0, E0])
        ohe0 = sb1("ohe0", [P, K0, E0])
        w0 = sb1("w0", [P, E0])
        exp1 = sb1("exp1", [P, E1])
        score = sb1("score", [P, 3, E1])
        top1 = sb1("top1", [P, 8])
        top1_i = sb1("top1_i", [P, 8], U32)
        sum1 = sb1("sum1", [P, 3])
        oh = sb1("oh", [P, K1, E1])
        ohr = sb1("ohr", [P, K1, E1])
        slot_f = sb1("slot_f", [P, K1])
        mask = sb1("mask", [P, 2, E1], F32R)
        rk = sb1("rk", [P, E1])
        rowno = sb1("rowno", [P, E1])

        iota_s = sb1("iota_s", [1, NS])
        ge = sb1("ge", [1, NS, E1])
        ts = sb1("ts", [1, 4, NS])
        first_use.close()

        wd_lo = sb("wd_lo", [P, NE * IC, D], F32R)
        row_t = sb("row_t", [P, V, ROW])
        tok_i = sb("tok_i", [P, U], U32)
        qx = sb("qx", [P, 2, NA, R])
        qxT = sb("qxT", [P, 2, P])
        sg = sb("sg", [P, 2, I1])
        z = sb("z", [P, 2, I1])
        zT_hi = sb("zT_hi", [P, 2, IC, P], F32R)
        zT_lo = sb("zT_lo", [P, 2, IC, P], F32R)
        y_sb = sb("y_sb", [P, U, D])
        behind = 3 * KC * GU - V * ROW - U - 2 * (NA * R + P + 2 * I1 + 2 * IC * P) - U * D
        sb("behind", [P, behind])
        wd_hi = sb("wd_hi", [P, NE * IC, D], F32R)
        sums = m_all[:, 0:ACC * V, :]

        s = {n: sem(n) for n in (
            "made", "consts", "small_in", "cond_row", "gl0_in", "base_w_in", "lb0_in", "ab_in", "aa_in",
            "split_hi", "split_lo", "gate_q_mm", "gate_q_ready", "ci_ready", "bd_ready", "xb_ready",
            "hwT_hi", "yT_mm", "yT_ready", "yT_hi", "yT_lo", "h_mm", "d_ready", "exp0", "r0_step", "hw_ready", "hwT_mm",
            "hwT_lo", "base_mm", "r_mm", "x1_ready", "x1T_mm", "x1T_ready", "q_mm", "q_ready", "q16_ready",
            "qT_mm", "qT_ready", "s_mm", "exp1", "r1_step", "w_ready", "mask_ready", "rank_mm", "rank_step",
            "rank_done", "row_step", "rows_ready", "wd_in", "zeros_out",
            "m_mm", "m_ready", "t_step", "pad_ready", "tables", "pads", "spare_out", "wd_hi", "wd_lo",
            "qx_ready", "qx_mm", "qxT_ready", "gu_mm", "silu", "z_ready", "zT_mm", "zT_hi", "zT_lo",
            "y_mm", "y_ready", "tok_ready", "sum_step", "out_ready",
            "dve_held", "pool_held")}

        def ring(name, n):
            return [sem(f"{name}{i}") for i in range(n)]

        x_in, w_in, x1_out, scat, t_out = (ring(n, U) for n in ("x_in", "w_in", "x1_out", "scat", "t_out"))
        st_in = ring("st_in", 3)
        row_in = ring("row_in", V)
        added = ring("added", U)
        a_in = ring("a_in", V)
        o_out = ring("o_out", V)

        Y, X1T, HT, H, R0, R1, Q, QT = bank
        RB = (R0, R1)
        FB = (H, Y, R0)
        rank_ps = HT[:, P:P + 2 * E1]
        s_ps = QT[:, P:P + E1]
        b_qx, b_gu, b_zT, b_y = Y, (X1T, HT), H, (Q, QT)

        def back(u, p, lag, n):
            d = p - lag
            return u + d // n, d % n

        def live(u, p, n, count):
            return not isinstance(u, int) or 0 <= n * u + p < count

        def late(u, p, n, k):
            return not isinstance(u, int) or n * u + p >= k

        def passes(eng, n, count, lag, lead, body, most_lead=None, after_lead=None):
            first = -(-(lag + n) // n)
            last = (count - (lead if most_lead is None else most_lead)) // n
            for i in range(-lead, first * n):
                body(i // n, i % n)
                if i == 0 and after_lead:
                    after_lead()
            with eng.Fori(first, last) as u:
                for p in range(n):
                    body(u, p)
            for i in range(last * n, count + lag):
                body(i // n, i % n)

        block = ctx.enter_context(nc.Block())

        @block.sync
        def _(sp):
            sp.dma_start(gl0_sb[:, :, :], gate_lora0).then_inc(s["gl0_in"], 16)
            sp.dma_start(stage[1], base_w).then_inc(s["base_w_in"], 16)

            def step(u, p):
                t = U * u + p
                if live(u, p, U, NT):
                    if late(u, p, U, U):
                        sp.wait_ge(s["x1_ready"], t - U + 1)
                    sp.dma_start(xt[:, p, :], xr[bass.ts(t, P), :]).then_inc(x_in[p], 16)
                    if isinstance(u, int) and t == 1:
                        sp.dma_start(lb0_sb[:, :], lora_b0).then_inc(s["lb0_in"], 16)
                        sp.dma_start(ab_sb[:, :, :], adapter_b).then_inc(s["ab_in"], 16)
                        sp.dma_start(aa_sb[:, :, :], adapter_a).then_inc(s["aa_in"], 16)
                        sp.dma_start(g1_sb[:, :, :], gate1).then_inc(s["aa_in"], 16)
                        sp.wait_ge(s["made"], 7)
                        sp.dma_start(acc[0][TOK:TOK + P, :], zero_tile[:, :]).then_inc(s["zeros_out"], 16)
                        sp.dma_start(acc[1][TOK:TOK + P, :], zero_tile[:, :]).then_inc(s["zeros_out"], 16)
                        sp.wait_ge(s["consts"], 5)
                        for n in range(SPARE):
                            sp.dma_start(q_rows[E1 * REGION + n * P:E1 * REGION + (n + 1) * P, :],
                                         pad_row[:, :]).then_inc(s["spare_out"], 16)
                v, w = back(u, p, 2, U)
                if live(v, w, U, NT):
                    sp.dma_start(wd_raw[:, bass.ds(U * v + w, 1), :], down[:, bass.ds(U * v + w, 1), :])\
                        .then_inc(s["wd_in"], 16)
                    sp.dma_start(acc[1][bass.ts(U * v + w, P), :], zero_tile[:, :]).then_inc(s["zeros_out"], 16)
                v, w = back(u, p, 6, U)
                if live(v, w, U, NT):
                    sp.wait_ge(s["x1_ready"], U * v + w + 1)
                    sp.dma_start(acc[0][bass.ts(U * v + w, P), :], x1[:, w, :]).then_inc(x1_out[w], 16)
                    sp.wait_ge(s["w_ready"], U * v + w + 1)
                    sp.dma_start(t_rows[bass.ts(U * v + w, P), :], rows[:, w, 0, :]).then_inc(t_out[w], 16)

            passes(sp, U, NT, 6, 0, step)
            for n in range(NT, NE * IC):
                sp.dma_start(wd_raw[:, n, :], down[:, n, :]).then_inc(s["wd_in"], 16)

            def load_stage(u, b):
                sp.wait_ge(s["m_mm"], 3 * u + b - 2)
                sp.dma_start(stage[b], gate_up[3 * u + b]).then_inc(st_in[b], 16)

            load_stage(1, 2)
            with sp.Fori(2, NE // 3) as u:
                for b in range(3):
                    load_stage(u, b)
            for e in range(NE // 3 * 3, NE):
                load_stage(e // 3, e % 3)

            sp.wait_ge(s["m_mm"], NE)
            sp.wait_ge(s["tables"], 2)
            sp.wait_ge(s["pads"], 16 * E1)
            sp.wait_ge(s["spare_out"], 16 * SPARE)
            for p in range(U):
                sp.wait_ge(scat[p], 16 * K1 * (NT // U))
                sp.wait_ge(t_out[p], 16 * (NT // U))

            def free_row(t, u, p, n):
                if late(u, p, V, V) or n:
                    sp.wait_ge(s["qx_ready"], t - V + 1)
                    sp.wait_ge(s["tok_ready"], t - V + 1)

            def tile_step(u, p):
                t = V * u + p
                free_row(t, u, p, 0)
                row = sp.value_load(tile_row[0:1, bass.ds(t, 1)], min_val=0, max_val=ROWS - P)
                sp.dma_start(row_t[:, p, :], q_rows[bass.ds(row, P), :]).then_inc(row_in[p], 16)

            passes(sp, V, NS, 0, 0, tile_step)

            def load_shared(u, p):
                t = V * u + p
                sp.wait_ge(s["qx_ready"], NS + t - V + 1)
                if isinstance(u, int) and t < V:
                    sp.wait_ge(s["tok_ready"], NS + t - V + 1)
                sp.dma_start(row_t[:, p, :], t_rows[bass.ts(t, P), :]).then_inc(row_in[p], 16)

            def load_sums(u, p):
                for a in range(ACC):
                    sp.dma_start(sums[:, 2 * p + a, :], acc[a][bass.ts(V * u + p, P), :]).then_inc(a_in[p], 16)

            def store_out(u, p):
                t = V * u + p
                sp.wait_ge(s["out_ready"], t + 1)
                sp.dma_start(outr[bass.ts(t, P), :], sums[:, 2 * p, :]).then_inc(o_out[p], 16)

            for p in range(V):
                load_shared(0, p)
            sp.wait_ge(s["gu_mm"], NS)
            for p in range(U):
                sp.wait_ge(added[p], 16 * (NS // U))

            def last_step(u, p):
                v, w = back(u, p, 1 - V, V)
                if live(v, w, V, NT) and late(u, p, V, 1):
                    load_shared(v, w)
                v, w = back(u, p, -AHEAD, V)
                if live(v, w, V, NT):
                    if late(v, w, V, V):
                        sp.wait_ge(o_out[w], 16 * v)
                    load_sums(v, w)
                v, w = back(u, p, 1, V)
                if live(v, w, V, NT):
                    store_out(v, w)

            passes(sp, V, NT, 1, AHEAD, last_step, V)
            for p in range(V):
                sp.wait_ge(o_out[p], 16 * (NT // V))

        @block.gpsimd
        def _(pool):
            def fill(dst, **how):
                return pool.iota(dst, allow_small_or_imprecise_dtypes=True, **how)

            pool.iota(part_i[:, :], pattern=[[0, 1]], base=0, channel_multiplier=1).then_inc(s["made"], 1)
            pool.memset(ident[:, :], 0.0).then_inc(s["made"], 1)
            pool.memset(ones[:, :], 1.0).then_inc(s["made"], 1)
            pool.memset(head[:, :, :], 0.0).then_inc(s["made"], 1)
            pool.memset(pad_row[:, :], 0.0).then_inc(s["made"], 1)
            pool.memset(zero_tile[:, :], 0.0).then_inc(s["made"], 1)
            fill(iota_e[:, :], pattern=[[1, E1]], base=0, channel_multiplier=0).then_inc(s["made"], 1)
            pool.wait_ge(s["made"], 7)
            pool.affine_select(out=diag[:, :, :], in_=ones[:, :].rearrange("p (b d) -> p b d", b=BPT),
                               compare_op=ALU.is_ge, fill=0.0, base=0, pattern=[[-SEQ, BPT], [0, SEQ]],
                               channel_multiplier=1).then_inc(s["consts"], 1)
            pool.wait_ge(s["consts"], 1)
            pool.affine_select(out=diag[:, :, :], in_=diag[:, :, :], compare_op=ALU.is_ge, fill=0.0,
                               base=SEQ - 1, pattern=[[SEQ, BPT], [0, SEQ]],
                               channel_multiplier=-1).then_inc(s["consts"], 1)
            pool.affine_select(out=ident[:, :], in_=ident[:, :], compare_op=ALU.not_equal, fill=1.0, base=0,
                               pattern=[[-1, P]], channel_multiplier=1).then_inc(s["consts"], 1)
            fill(pad_row[:, T_COL:T_COL + 1], pattern=[[0, 1]], base=TOK, channel_multiplier=1)\
                .then_inc(s["consts"], 1)
            fill(head[:, :, T_COL - R], pattern=[[P, NT]], base=0, channel_multiplier=1).then_inc(s["consts"], 1)
            pool.wait_ge(s["cond_row"], 1)

            def gather_cond(u, p):
                if late(u, p, U, U):
                    pool.wait_ge(s["bd_ready"], U * u + p - U + 1)
                pool.tensor_copy(cidx[:, p:p + 1], cond_row[:, bass.ds(U * u + p, 1)]).then_inc(s["ci_ready"], 1)
                pool.wait_ge(s["ci_ready"], U * u + p + 1)
                pool.sem_inc(s["pool_held"])
                pool.indirect_dma_start(
                    out=wrow[:, p, :], out_offset=None, in_=cond_w,
                    in_offset=bass.IndirectOffsetOnAxis(ap=cidx[:, p:p + 1], axis=0)).then_inc(w_in[p], 16)

            def step(u, p):
                v, w = back(u, p, -1, U)
                if live(v, w, U, NT):
                    gather_cond(v, w)
                if isinstance(u, int) and U * u + p == -1:
                    fill(iota_a[:, :, :], pattern=[[1, NA], [0, R]], base=0, channel_multiplier=0)\
                        .then_inc(s["consts"], 1)
                    fill(region_f[:, :], pattern=[[REGION, E1]], base=0, channel_multiplier=0)\
                        .then_inc(s["consts"], 1)
                    fill(iota_s[:, :], pattern=[[1, NS]], base=0, channel_multiplier=0).then_inc(s["consts"], 1)
                    pool.affine_select(out=tri[:, :], in_=ones[:, :], compare_op=ALU.is_gt, fill=0.0, base=0,
                                       pattern=[[1, P]], channel_multiplier=-1).then_inc(s["consts"], 1)
                if live(u, p, U, NT):
                    t = U * u + p
                    pool.wait_ge(w_in[p], 16 * u + 16)
                    if late(u, p, U, 2):
                        pool.wait_ge(s["yT_mm"], t - 1)
                    pool.tensor_tensor(bd[:, p % 2, :, :], wrow[:, p:p + 1, :].broadcast_to([P, BPT, SEQ]),
                                       diag[:, :, :], ALU.mult).then_inc(s["bd_ready"], 1)
                v, w = back(u, p, 6, U)
                if live(v, w, U, NT):
                    pool.wait_ge(s["w_ready"], U * v + w + 1)
                    pool.wait_ge(s["rank_step"], 4 * (U * v + w + 1))
                    pool.sem_inc(s["pool_held"])
                    for k in range(K1):
                        pool.indirect_dma_start(
                            out=q_rows, out_offset=bass.IndirectOffsetOnAxis(ap=slot_i[:, w, k:k + 1], axis=0),
                            in_=rows[:, w, k, :], in_offset=None).then_inc(scat[w], 16)

            passes(pool, U, NT, 6, 1, step)
            pool.wait_ge(s["pad_ready"], 1)
            for e in range(E1):
                pool.indirect_dma_start(
                    out=q_rows, out_offset=bass.IndirectOffsetOnAxis(ap=pad_i[:, e:e + 1], axis=0),
                    in_=pad_row[:, :], in_offset=None).then_inc(s["pads"], 16)
            for p in range(U):
                pool.wait_ge(x1_out[p], 16 * (NT // U))
            pool.wait_ge(s["zeros_out"], 16 * (NT + 2))

            def add_step(u, p):
                t = V * u + p
                v, w = back(u, p, ACC, V)
                if late(u, p, V, ACC):
                    pool.wait_ge(added[w % U], 16 * (V // U * v + w // U) + 16)
                pool.wait_ge(s["tok_ready"], t + 1)
                pool.wait_ge(s["y_ready"], t + 1)
                pool.sem_inc(s["pool_held"])
                pool.indirect_dma_start(
                    out=acc[p % ACC], out_offset=bass.IndirectOffsetOnAxis(ap=tok_i[:, p % U:p % U + 1], axis=0),
                    in_=y_sb[:, p % U, :], in_offset=None, compute_op=ALU.add).then_inc(added[p % U], 16)

            passes(pool, V, NS, 0, 0, add_step)

        @block.scalar
        def _(act):
            for b in range(BPT):
                act.dma_start(cond_i[b * SEQ:(b + 1) * SEQ, :], cond[b:b + 1, :].broadcast_to([SEQ, NT]))\
                    .then_inc(s["small_in"], 16)
                act.dma_start(adapter_i[b * SEQ:(b + 1) * SEQ, :], adapters[b:b + 1, :].broadcast_to([SEQ, NT]))\
                    .then_inc(s["small_in"], 16)
            act.dma_start(base_b_sb[:, :], base_b.rearrange("(a d) -> a d", a=1).broadcast_to([P, D]))\
                .then_inc(s["small_in"], 16)
            act.dma_start(bias_sb[:, :], bias1.rearrange("(a d) -> a d", a=1).broadcast_to([P, E1]))\
                .then_inc(s["small_in"], 16)
            act.wait_ge(s["base_w_in"], 16)
            act.copy(base_w_hi[:, :, :], stage[1]).then_inc(s["split_hi"], 1)
            act.dma_start(stage[0], gate_up[0]).then_inc(st_in[0], 16)
            act.wait_ge(s["split_lo"], 1)
            act.wait_ge(s["split_hi"], 1)
            act.dma_start(stage[1], gate_up[1]).then_inc(st_in[1], 16)

            def load_stage(e):
                act.dma_start(stage[e % 3], gate_up[e]).then_inc(st_in[e % 3], 16)

            def fold(u, b):
                e = 3 * u + b
                act.wait_ge(s["m_mm"], e + 1)
                act.copy(m_all[:, e, :] if isinstance(u, int) else
                         m_all[:, bass.ds(e, 1), :].rearrange("p a n -> p (a n)"), FB[b][:, :])\
                    .then_inc(s["m_ready"], 1)

            def step(u, p):
                if isinstance(u, int) and U * u + p == NT:
                    act.wait_ge(s["base_mm"], NT)
                    load_stage(2)
                if isinstance(u, int) and U * u + p > NT:
                    e = U * u + p - NT - 1
                    fold(0, e)
                    load_stage(e + 3)
                v, w = back(u, p, 3, U)
                if live(v, w, U, NT):
                    t = U * v + w
                    act.wait_ge(s["qT_mm"], t + 1)
                    if late(v, w, U, 1):
                        act.wait_ge(s["s_mm"], t)
                    act.copy(qT[:, :], QT[:, 0:P]).then_inc(s["qT_ready"], 1)
                v, w = back(u, p, 1, U)
                if live(v, w, U, NT):
                    t = U * v + w
                    act.wait_ge(s["hwT_mm"], t + 1)
                    if late(v, w, U, 1):
                        act.wait_ge(s["r_mm"], t)
                    act.copy(hwT_hi[:, :], HT[:, 0:P]).then_inc(s["hwT_hi"], 1)
                if live(u, p, U, NT):
                    act.wait_ge(s["d_ready"], U * u + p + 1)
                    act.activation(exp0[:, :], d0[:, :], ACT.Exp, accum_out=sum0[:, 0:1]).then_inc(s["exp0"], 1)
                v, w = back(u, p, -1, U)
                if live(v, w, U, NT):
                    t = U * v + w
                    act.wait_ge(s["yT_mm"], t + 1)
                    if late(v, w, U, 2):
                        act.wait_ge(s["base_mm"], t - 1)
                    act.copy(yT[:, w % 2, :, :].rearrange("p c t -> p (c t)"), Y[:, :]).then_inc(s["yT_ready"], 1)
                    act.copy(yT_hi[:, w % 2, :, :].rearrange("p c t -> p (c t)"), Y[:, :]).then_inc(s["yT_hi"], 1)
                v, w = back(u, p, 2, U)
                if live(v, w, U, NT):
                    t = U * v + w
                    act.wait_ge(s["x1T_mm"], t + 1)
                    if late(v, w, U, 1):
                        act.wait_ge(s["q_mm"], t)
                    act.copy(x1T[:, :, :].rearrange("p c t -> p (c t)"), X1T[:, :]).then_inc(s["x1T_ready"], 1)
                v, w = back(u, p, 3, U)
                if live(v, w, U, NT):
                    t = U * v + w
                    act.wait_ge(s["q16_ready"], t + 1)
                    if late(v, w, U, U):
                        act.wait_ge(scat[w], 16 * K1 * v)
                        act.wait_ge(t_out[w], 16 * v)
                    act.copy(rows[:, w, :, 0:R], q16[:, w, :, :].broadcast_to([P, K1, R]))\
                        .then_inc(s["row_step"], 1)
                    act.copy(rows[:, w, :, R:ROW], head[:, bass.ds(t, 1), :].broadcast_to([P, K1, ROW - R]))\
                        .then_inc(s["rows_ready"], 1)
                    act.wait_ge(s["s_mm"], t + 1)
                    if late(v, w, U, 1):
                        act.wait_ge(s["mask_ready"], t)
                    act.activation(exp1[:, :], s_ps, ACT.Exp, scale=-1.0).then_inc(s["exp1"], 1)

            def first_gate():
                act.wait_ge(s["gate_q_mm"], 1)
                act.copy(gate_q[:, :], Q[:, 0:E1]).then_inc(s["gate_q_ready"], 1)

            passes(act, U, NT, 3, 1, step, after_lead=first_gate)

            def high(e):
                act.copy(wd_hi[:, bass.ds(2 * e, 2), :], wd_raw[:, bass.ds(2 * e, 2), :]).then_inc(s["wd_hi"], 1)

            fold(0, 2)
            with act.Fori(1, 3) as u:
                for b in range(3):
                    fold(u, b)
            act.wait_ge(s["wd_in"], 16 * NE * IC)
            act.wait_ge(s["tables"], 2)
            act.wait_ge(s["zeros_out"], 16 * (NT + 2))
            act.wait_ge(s["row_step"], NT)
            act.wait_ge(s["rows_ready"], NT)
            for p in range(U):
                act.wait_ge(scat[p], 16 * K1 * (NT // U))
                act.wait_ge(x1_out[p], 16 * (NT // U))
                act.wait_ge(t_out[p], 16 * (NT // U))
            with act.Fori(3, NE // 3) as u:
                for b in range(3):
                    fold(u, b)
                    high(6 * u + 2 * b - 18)
                    high(6 * u + 2 * b - 17)
            for e in range(NE // 3 * 3, NE):
                fold(e // 3, e % 3)
                high(2 * e - 18)
                high(2 * e - 17)
            high(NE - 1)

            def silu(t, i, p):
                act.wait_ge(s["gu_mm"], t + 1)
                if i is None or i >= 2:
                    act.wait_ge(s["z_ready"], t - 1)
                act.activation(sg[:, p % 2, :], b_gu[p % 2][:, 0:I1], ACT.Silu).then_inc(s["silu"], 1)

            def zT_high(t, i, p):
                act.wait_ge(s["zT_mm"], t + 1)
                if i is None or i >= 2:
                    act.wait_ge(s["y_mm"], t - 1)
                act.copy(zT_hi[:, p % 2, :, :].rearrange("p c t -> p (c t)"), b_zT[:, 0:I1]).then_inc(s["zT_hi"], 1)

            def turned(t, i, p):
                act.wait_ge(s["qx_mm"], t + 1)
                if i is None or i >= 2:
                    act.wait_ge(s["gu_mm"], t - 1)
                act.copy(qxT[:, p % 2, :], b_qx[:, 0:P]).then_inc(s["qxT_ready"], 1)

            def index(u, p):
                return V * u + p if isinstance(u, int) else None

            def tile_step(u, p):
                t = V * u + p
                if live(u, p, V, NS):
                    silu(t, index(u, p), p)
                v, w = back(u, p, 1, V)
                if live(v, w, V, NS):
                    zT_high(V * v + w, index(v, w), w)
                v, w = back(u, p, -1, V)
                if live(v, w, V, NS):
                    turned(V * v + w, index(v, w), w)
                v, w = back(u, p, 2, V)
                if live(v, w, V, NS):
                    act.wait_ge(s["y_mm"], V * v + w + 1)
                    if late(v, w, V, U):
                        act.wait_ge(added[w % U], 16 * (V // U * v + w // U))
                    act.activation(y_sb[:, w % U, :], b_y[w % 2][:, :], ACT.Copy, scale=row_t[:, w, W_COL:W_COL + 1])\
                        .then_inc(s["y_ready"], 1)

            passes(act, V, NS, 2, 1, tile_step)

            def last_step(u, p):
                t = NS + V * u + p
                if live(u, p, V, NT):
                    silu(t, None, p)
                v, w = back(u, p, 1, V)
                if live(v, w, V, NT):
                    zT_high(NS + V * v + w, None, w)
                v, w = back(u, p, -1, V)
                if live(v, w, V, NT):
                    turned(NS + V * v + w, None, w)

            passes(act, V, NT, 1, 1, last_step)

        @block.tensor
        def _(pe):
            def mm(o, lhsT, rhs, start, stop):
                return pe.matmul(o, lhsT, rhs, start=start, stop=stop)

            def mm_split(o, left, right, start, stop):
                mm(o, left[0], right[0], start, False)
                mm(o, left[1], right[0], False, False)
                return mm(o, left[0], right[1], False, stop)

            def fold(u, b):
                e = 3 * u + b
                if not isinstance(u, int) or e >= 3:
                    pe.wait_ge(s["m_ready"], e - 2)
                elif b == 0:
                    pe.wait_ge(s["hw_ready"], NT)
                elif b == 1:
                    pe.wait_ge(s["yT_lo"], NT)
                else:
                    pe.wait_ge(s["x1_ready"], NT)
                pe.wait_ge(st_in[b], 16 * u + 16)
                for c in range(KC):
                    last = mm(FB[b][:, :], aa_sb[:, c, :], stage[b][:, c, :], c == 0, c == KC - 1)
                last.then_inc(s["m_mm"], 1)

            def step(u, p):
                if isinstance(u, int) and U * u + p >= NT:
                    fold((U * u + p - NT) // 3, (U * u + p - NT) % 3)
                if live(u, p, U, NT):
                    t = U * u + p
                    pe.wait_ge(s["yT_ready"], t + 1)
                    if isinstance(u, int) and t == 0:
                        pe.wait_ge(s["gl0_in"], 16)
                    if late(u, p, U, 1):
                        pe.wait_ge(s["hw_ready"], t)
                    for c in range(KC):
                        last = mm(H[:, 0:E0 + E0 * R], yT[:, p % 2, c, :], gl0_sb[:, c, :], c == 0, c == KC - 1)
                    last.then_inc(s["h_mm"], 1)
                v, w = back(u, p, 3, U)
                if live(v, w, U, NT):
                    t = U * v + w
                    pe.wait_ge(s["q_ready"], t + 1)
                    if late(v, w, U, 1):
                        pe.wait_ge(s["exp1"], t)
                    pe.transpose(QT[:, 0:P], q_sb[:, :, :].rearrange("p a r -> p (a r)"), ident[:, :])\
                        .then_inc(s["qT_mm"], 1)
                v, w = back(u, p, -1, U)
                if live(v, w, U, NT):
                    t = U * v + w
                    pe.wait_ge(x_in[w], 16 * v + 16)
                    pe.wait_ge(s["bd_ready"], t + 1)
                    if late(v, w, U, 1):
                        pe.wait_ge(s["yT_lo"], t)
                    for c in range(KC):
                        last = mm(Y[:, c * P:(c + 1) * P], xt[:, w, c * P:(c + 1) * P],
                                  bd[:, w % 2, :, :].rearrange("p b d -> p (b d)"), True, True)
                    last.then_inc(s["yT_mm"], 1)
                v, w = back(u, p, 1, U)
                if live(v, w, U, NT):
                    t = U * v + w
                    pe.wait_ge(s["hw_ready"], t + 1)
                    if late(v, w, U, 1):
                        pe.wait_ge(s["hwT_lo"], t)
                    if late(v, w, U, 4):
                        pe.wait_ge(s["rank_done"], t - 3)
                    pe.transpose(HT[:, 0:P], hw[:, :, :].rearrange("p e r -> p (e r)"), ident[:, :])\
                        .then_inc(s["hwT_mm"], 1)
                v, w = back(u, p, 2, U)
                if live(v, w, U, NT):
                    t = U * v + w
                    pe.wait_ge(s["x1_ready"], t + 1)
                    if late(v, w, U, 1):
                        pe.wait_ge(s["x1T_ready"], t)
                    for c in range(KC):
                        last = pe.transpose(X1T[:, c * P:(c + 1) * P], x1[:, w, c * P:(c + 1) * P], ident[:, :])
                    last.then_inc(s["x1T_mm"], 1)
                if live(u, p, U, NT):
                    t = U * u + p
                    pe.wait_ge(s["yT_lo"], t + 1)
                    if isinstance(u, int) and t == 0:
                        pe.wait_ge(s["split_hi"], 1)
                        pe.wait_ge(s["split_lo"], 1)
                    if late(u, p, U, 2):
                        pe.wait_ge(s["x1_ready"], t - 1)
                    for c in range(KC):
                        last = mm_split(RB[p % 2][:, :], (yT_hi[:, p % 2, c, :], yT_lo[:, p % 2, c, :]),
                                        (base_w_hi[:, c, :], base_w_lo[:, c, :]), c == 0, False)
                    last.then_inc(s["base_mm"], 1)
                v, w = back(u, p, 4, U)
                if live(v, w, U, NT):
                    t = U * v + w
                    pe.wait_ge(s["mask_ready"], t + 1)
                    pe.wait_ge(s["hwT_lo"], min(t + 4, NT) if isinstance(u, int) else t + 4)
                    mm(rank_ps[:, 0:E1], tri_r[:, :], mask[:, w % 2, :], True, True)
                    mm(rank_ps[:, E1:2 * E1], ones_r[:, :], mask[:, w % 2, :], True, True).then_inc(s["rank_mm"], 1)
                v, w = back(u, p, 3, U)
                if live(v, w, U, NT):
                    pe.wait_ge(s["qT_ready"], U * v + w + 1)
                    mm(s_ps, qT[:, :], gate_q[:, :], True, True).then_inc(s["s_mm"], 1)
                v, w = back(u, p, 2, U)
                if live(v, w, U, NT):
                    t = U * v + w
                    pe.wait_ge(s["x1T_ready"], t + 1)
                    if isinstance(u, int) and t == 0:
                        pe.wait_ge(s["ab_in"], 16)
                        pe.wait_ge(s["gate_q_ready"], 1)
                    if late(v, w, U, 1):
                        pe.wait_ge(s["q_ready"], t)
                    for c in range(KC):
                        last = mm(Q[:, 0:P], x1T[:, c, :], ab_sb[:, c, :], c == 0, c == KC - 1)
                    last.then_inc(s["q_mm"], 1)
                v, w = back(u, p, 1, U)
                if live(v, w, U, NT):
                    t = U * v + w
                    pe.wait_ge(s["hwT_lo"], t + 1)
                    if isinstance(u, int) and t == 0:
                        pe.wait_ge(s["split_lo"], 2)
                    mm_split(RB[w % 2][:, :], (hwT_hi[:, :], hwT_lo[:, :]), (lb0_hi[:, :], lb0_lo[:, :]),
                             False, True).then_inc(s["r_mm"], 1)

            def first_gate():
                pe.wait_ge(s["aa_in"], 32)
                for c in range(KC):
                    last = mm(Q[:, 0:E1], aa_sb[:, c, :], g1_sb[:, c, :], c == 0, c == KC - 1)
                last.then_inc(s["gate_q_mm"], 1)

            pe.wait_ge(s["consts"], 9)
            passes(pe, U, NT, 4, 1, step, after_lead=first_gate)

            for e in (4, 5):
                fold(1, e - 3)
            with pe.Fori(2, NE // 3) as u:
                for b in range(3):
                    fold(u, b)
            for e in range(NE // 3 * 3, NE):
                fold(e // 3, e % 3)

            pe.wait_ge(s["m_ready"], NE)
            pe.wait_ge(s["tables"], 2)
            pe.wait_ge(s["rank_done"], NT)
            pe.wait_ge(s["exp1"], NT)

            def part(tensor, e, c, n):
                if isinstance(e, int):
                    return tensor[:, n * e + c, :]
                return tensor[:, bass.ds(e * n + c, 1), :].rearrange("p a n -> p (a n)")

            def gate_up_product(t, i, p, e):
                pe.wait_ge(s["qxT_ready"], t + 1)
                if i is None or i >= 2:
                    pe.wait_ge(s["z_ready"], t - 1)
                mm(b_gu[p % 2][:, :], qxT[:, p % 2, :], part(m_all, e, 0, 1), True, True).then_inc(s["gu_mm"], 1)

            def turn_z(t, i, p):
                pe.wait_ge(s["z_ready"], t + 1)
                if i is None or i >= 1:
                    pe.wait_ge(s["zT_lo"], t)
                for c in range(IC):
                    last = pe.transpose(b_zT[:, c * P:(c + 1) * P], z[:, p % 2, c * P:(c + 1) * P], ident[:, :])
                last.then_inc(s["zT_mm"], 1)

            def turn_q(t, i, p):
                pe.wait_ge(s["qx_ready"], t + 1)
                if i is None or i >= 1:
                    pe.wait_ge(s["qxT_ready"], t)
                pe.transpose(b_qx[:, 0:P], qx[:, p % 2, :, :].rearrange("p a r -> p (a r)"), ident[:, :])\
                    .then_inc(s["qx_mm"], 1)

            def down_product(t, p, e, free):
                pe.wait_ge(s["zT_lo"], t + 1)
                free()
                for c in range(IC):
                    last = mm_split(b_y[p % 2][:, :], (zT_hi[:, p % 2, c, :], zT_lo[:, p % 2, c, :]),
                                    (part(wd_hi, e, c, IC), part(wd_lo, e, c, IC)), c == 0, c == IC - 1)
                last.then_inc(s["y_mm"], 1)

            def expert_of(t):
                return pe.value_load(tile_e[0:1, bass.ds(t, 1)], min_val=0, max_val=NE - 1)

            loaded = {}

            def index(u, p):
                return V * u + p if isinstance(u, int) else None

            def tile_step(u, p):
                if p == 0:
                    loaded.clear()
                if live(u, p, V, NS):
                    loaded[p] = expert_of(V * u + p)
                    gate_up_product(V * u + p, index(u, p), p, loaded[p])
                v, w = back(u, p, 1, V)
                if live(v, w, V, NS):
                    turn_z(V * v + w, index(v, w), w)
                v, w = back(u, p, -1, V)
                if live(v, w, V, NS):
                    turn_q(V * v + w, index(v, w), w)
                v, w = back(u, p, 2, V)
                if live(v, w, V, NS):
                    t = V * v + w

                    def free():
                        if late(v, w, V, 2):
                            pe.wait_ge(s["y_ready"], t - 1)
                        elif w == 0:
                            pe.wait_ge(s["wd_hi"], NE)
                            pe.wait_ge(s["wd_lo"], NE)

                    down_product(t, w, loaded[w] if w in loaded else expert_of(t), free)

            passes(pe, V, NS, 2, 1, tile_step)

            def last_step(u, p):
                if live(u, p, V, NT):
                    gate_up_product(NS + V * u + p, None, p, NE - 1)
                v, w = back(u, p, 1, V)
                if live(v, w, V, NT):
                    turn_z(NS + V * v + w, None, w)
                v, w = back(u, p, -1, V)
                if live(v, w, V, NT):
                    turn_q(NS + V * v + w, None, w)
                v, w = back(u, p, 2, V)
                if live(v, w, V, NT):
                    t = V * v + w

                    def free():
                        if late(v, w, V, 2):
                            pe.wait_ge(s["sum_step"], t - 1)
                        else:
                            pe.wait_ge(s["y_ready"], NS + t - 1)

                    down_product(NS + t, w, NE - 1, free)

            passes(pe, V, NT, 2, 1, last_step)

        @block.vector
        def _(dve):
            def low(out_, exact, high, what):
                dve.tensor_tensor(out_, exact, high.bitcast(F32), ALU.subtract).then_inc(s[what], 1)

            dve.wait_ge(s["made"], 4)
            dve.tensor_scalar(c_i[:, :], part_i[:, :], SEQ - 1, None, ALU.bitwise_and).then_inc(s["t_step"], 1)
            dve.wait_ge(s["t_step"], 1)
            dve.tensor_copy(c_f[:, :], c_i[:, :]).then_inc(s["t_step"], 1)
            dve.tensor_copy(part_f[:, :], part_i[:, :]).then_inc(s["t_step"], 1)
            dve.wait_ge(s["small_in"], 16 * (2 * BPT + 2))
            dve.wait_ge(s["t_step"], 3)
            dve.tensor_scalar(cond_row[:, :], cond_i[:, :], float(SEQ), c_f[:, 0:1], ALU.mult, ALU.add)\
                .then_inc(s["cond_row"], 1)
            dve.tensor_copy(head[:, :, A_COL - R], adapter_i[:, :]).then_inc(s["t_step"], 1)
            dve.wait_ge(s["split_hi"], 1)
            low(base_w_lo[:, :, :], stage[1], base_w_hi[:, :, :], "split_lo")
            dve.wait_ge(s["consts"], 9)
            dve.tensor_copy(rowno[:, :], region_f[:, :]).then_inc(s["t_step"], 1)
            dve.tensor_copy(tri_r[:, :], tri[:, :]).then_inc(s["t_step"], 1)
            dve.tensor_copy(ones_r[:, :], ones[:, :]).then_inc(s["t_step"], 1)
            dve.wait_ge(s["lb0_in"], 16)
            dve.tensor_copy(lb0_hi[:, :], lb0_sb[:, :]).then_inc(s["t_step"], 1)
            dve.wait_ge(s["t_step"], 8)
            low(lb0_lo[:, :], lb0_sb[:, :], lb0_hi[:, :], "split_lo")

            def routing(zero, one, rank):
                live0, live1, live_rank = (live(*tile, U, NT) for tile in (zero, one, rank))
                (u0, p0), (u1, p1), (u2, p2) = zero, one, rank
                t0, t1, t2 = U * u0 + p0, U * u1 + p1, U * u2 + p2
                at0, at1, at2 = 6 * t0, 9 * t1, 4 * t2

                if live_rank:
                    dve.wait_ge(s["rank_mm"], t2 + 1)
                    dve.tensor_tensor(rk[:, :], rank_ps[:, 0:E1], rowno[:, :], ALU.add).then_inc(s["rank_step"], 1)
                if live1:
                    dve.wait_ge(s["exp1"], t1 + 1)
                    dve.tensor_scalar(score[:, 0, :], exp1[:, :], 1.0, None, ALU.add).then_inc(s["r1_step"], 1)
                if live_rank:
                    dve.wait_ge(s["rank_step"], at2 + 1)
                    dve.tensor_tensor(rowno[:, :], rowno[:, :], rank_ps[:, E1:2 * E1], ALU.add)\
                        .then_inc(s["rank_done"], 1)
                    dve.tensor_tensor(ohr[:, :, :], oh[:, :, :],
                                      rk[:, :].rearrange("p (a e) -> p a e", a=1).broadcast_to([P, K1, E1]),
                                      ALU.mult).then_inc(s["rank_step"], 1)
                if live1:
                    dve.wait_ge(s["r1_step"], at1 + 1)
                    dve.reciprocal(score[:, 1, :], score[:, 0, :]).then_inc(s["r1_step"], 1)
                if live0:
                    dve.wait_ge(s["h_mm"], t0 + 1)
                    dve.sem_inc(s["dve_held"])
                    dve.max(top0[:, :], H[:, 0:E0]).then_inc(s["r0_step"], 1)
                if live_rank:
                    dve.wait_ge(s["rank_step"], at2 + 2)
                    dve.tensor_reduce(slot_f[:, :], ohr[:, :, :], AX.X, ALU.add).then_inc(s["rank_step"], 1)
                if live1:
                    dve.wait_ge(s["r1_step"], at1 + 2)
                    dve.tensor_tensor(score[:, 2, :], score[:, 1, :], bias_sb[:, :], ALU.add)\
                        .then_inc(s["r1_step"], 1)
                if live0:
                    dve.wait_ge(s["r0_step"], at0 + 1)
                    dve.tensor_scalar(d0[:, :], top0[:, 0:K0], top0[:, 0:1], None, ALU.subtract)\
                        .then_inc(s["d_ready"], 1)
                    dve.sem_inc(s["dve_held"])
                    dve.max_index(top0_i[:, :], top0[:, :], H[:, 0:E0]).then_inc(s["r0_step"], 1)
                if live1:
                    if late(u1, p1, U, 1):
                        dve.wait_ge(s["w_ready"], t1)
                    dve.wait_ge(s["r1_step"], at1 + 3)
                    dve.sem_inc(s["dve_held"])
                    dve.max(top1[:, :], score[:, 2, :]).then_inc(s["r1_step"], 1)
                if live_rank:
                    if late(u2, p2, U, U):
                        dve.wait_ge(scat[p2], 16 * K1 * u2)
                    dve.wait_ge(s["rank_step"], at2 + 3)
                    dve.tensor_copy(slot_i[:, p2, :], slot_f[:, :]).then_inc(s["rank_step"], 1)
                if live0:
                    dve.wait_ge(s["r0_step"], at0 + 2)
                    dve.tensor_tensor(
                        oh0[:, :, :], iota_e[:, 0:E0].rearrange("p (a e) -> p a e", a=1).broadcast_to([P, K0, E0]),
                        top0_i[:, 0:K0].rearrange("p (k a) -> p k a", a=1).broadcast_to([P, K0, E0]),
                        ALU.is_equal).then_inc(s["r0_step"], 1)
                if live1:
                    dve.wait_ge(s["r1_step"], at1 + 4)
                    dve.sem_inc(s["dve_held"])
                    dve.max_index(top1_i[:, :], top1[:, :], score[:, 2, :]).then_inc(s["r1_step"], 1)
                    dve.tensor_reduce(sum1[:, 0:1], top1[:, 0:K1], AX.X, ALU.add).then_inc(s["r1_step"], 1)
                if live0:
                    dve.wait_ge(s["exp0"], t0 + 1)
                    dve.wait_ge(s["r0_step"], at0 + 3)
                    dve.tensor_tensor(ohe0[:, :, :], oh0[:, :, :],
                                      exp0[:, :].rearrange("p (k a) -> p k a", a=1).broadcast_to([P, K0, E0]),
                                      ALU.mult).then_inc(s["r0_step"], 1)
                    dve.reciprocal(sum0[:, 1:2], sum0[:, 0:1]).then_inc(s["r0_step"], 1)
                if live1:
                    if live_rank:
                        dve.wait_ge(s["rank_step"], at2 + 3)
                    dve.wait_ge(s["r1_step"], at1 + 6)
                    dve.tensor_tensor(
                        oh[:, :, :], iota_e[:, :].rearrange("p (a e) -> p a e", a=1).broadcast_to([P, K1, E1]),
                        top1_i[:, 0:K1].rearrange("p (k a) -> p k a", a=1).broadcast_to([P, K1, E1]),
                        ALU.is_equal).then_inc(s["r1_step"], 1)
                    dve.tensor_scalar(sum1[:, 1:2], sum1[:, 0:1], 1e-20, None, ALU.add).then_inc(s["r1_step"], 1)
                if live0:
                    dve.wait_ge(s["r0_step"], at0 + 5)
                    dve.tensor_reduce(w0[:, :], ohe0[:, :, :].rearrange("p k e -> p e k"), AX.X, ALU.add)\
                        .then_inc(s["r0_step"], 1)
                if live1:
                    dve.wait_ge(s["r1_step"], at1 + 8)
                    with nc.allow_low_precision(reason="sums of a few 0s and at most one 1 are exact"):
                        dve.tensor_reduce(mask[:, p1 % 2, :], oh[:, :, :].rearrange("p k e -> p e k"), AX.X,
                                          ALU.add).then_inc(s["mask_ready"], 1)
                    dve.reciprocal(sum1[:, 2:3], sum1[:, 1:2]).then_inc(s["r1_step"], 1)
                if live0:
                    if late(u0, p0, U, 1):
                        dve.wait_ge(s["hwT_mm"], t0)
                    dve.wait_ge(s["r0_step"], at0 + 6)
                    dve.scalar_tensor_tensor(
                        out=hw[:, :, :], in0=H[:, E0:E0 + E0 * R].rearrange("p (e r) -> p e r", e=E0),
                        scalar=sum0[:, 1:2],
                        in1=w0[:, :].rearrange("p (e a) -> p e a", a=1).broadcast_to([P, E0, R]),
                        op0=ALU.mult, op1=ALU.mult).then_inc(s["hw_ready"], 1)
                if live1:
                    dve.wait_ge(s["rows_ready"], t1 + 1)
                    dve.wait_ge(s["r1_step"], at1 + 9)
                    dve.tensor_scalar(rows[:, p1, :, W_COL], top1[:, 0:K1], sum1[:, 2:3], None, ALU.mult)\
                        .then_inc(s["w_ready"], 1)

            def step(u, p):
                v, w = back(u, p, 2, U)
                if live(v, w, U, NT):
                    dve.wait_ge(s["xb_ready"], U * v + w + 1)
                    dve.wait_ge(s["r_mm"], U * v + w + 1)
                    if late(v, w, U, U):
                        dve.wait_ge(x1_out[w], 16 * v)
                    dve.tensor_tensor(x1[:, w, :], RB[w % 2][:, :], xt[:, w, :], ALU.add)\
                        .then_inc(s["x1_ready"], 1)
                routing((u, p), back(u, p, 4, U), back(u, p, 5, U))
                v, w = back(u, p, 1, U)
                if live(v, w, U, NT):
                    dve.wait_ge(s["hwT_hi"], U * v + w + 1)
                    if late(v, w, U, 1):
                        dve.wait_ge(s["r_mm"], U * v + w)
                    low(hwT_lo[:, :], HT[:, 0:P], hwT_hi[:, :], "hwT_lo")
                    dve.wait_ge(s["yT_mm"], U * v + w + 1)
                    dve.tensor_tensor(xt[:, w, :], xt[:, w, :], base_b_sb[:, :], ALU.add).then_inc(s["xb_ready"], 1)
                v, w = back(u, p, -1, U)
                if live(v, w, U, NT):
                    dve.wait_ge(s["yT_hi"], U * v + w + 1)
                    low(yT_lo[:, w % 2, :, :].rearrange("p c t -> p (c t)"), Y[:, :],
                        yT_hi[:, w % 2, :, :].rearrange("p c t -> p (c t)"), "yT_lo")
                v, w = back(u, p, 2, U)
                if live(v, w, U, NT):
                    t = U * v + w
                    dve.wait_ge(s["q_mm"], t + 1)
                    if late(v, w, U, 1):
                        dve.wait_ge(s["qT_mm"], t)
                        dve.wait_ge(s["q16_ready"], t)
                    dve.scalar_tensor_tensor(
                        out=q_sb[:, :, :].rearrange("p a r -> p (a r)"),
                        in0=iota_a[:, :, :].rearrange("p a r -> p (a r)"),
                        scalar=head[:, bass.ds(t, 1), A_COL - R:A_COL - R + 1].rearrange("p a r -> p (a r)"),
                        in1=Q[:, 0:P], op0=ALU.is_equal, op1=ALU.mult).then_inc(s["q_ready"], 1)
                    if late(v, w, U, U):
                        dve.wait_ge(s["rows_ready"], t - U + 1)
                    dve.wait_ge(s["q_ready"], t + 1)
                    dve.tensor_reduce(q16[:, w, 0, :], q_sb[:, :, :].rearrange("p a r -> p r a"), AX.X, ALU.add)\
                        .then_inc(s["q16_ready"], 1)

            passes(dve, U, NT, 5, 1, step)

            n = [8]

            def link(ins):
                ins.then_inc(s["t_step"], 1)
                n[0] += 1
                dve.wait_ge(s["t_step"], n[0])

            dve.wait_ge(s["rank_done"], NT)
            dve.tensor_scalar(pad_i[:, :], rowno[:, :], part_f[:, 0:1], None, ALU.add).then_inc(s["pad_ready"], 1)
            link(dve.tensor_tensor(tf[:, 0, :], rowno[:, :], region_f[:, :], ALU.subtract))
            link(dve.tensor_scalar(ti[:, 0, :], tf[:, 0, :], float(P - 1), None, ALU.add))
            link(dve.tensor_scalar(ti[:, 1, :], ti[:, 0, :], P.bit_length() - 1, None, ALU.arith_shift_right))
            link(dve.tensor_copy(tf[:, 1, :], ti[:, 1, :]))
            link(dve.tensor_copy(tf[:, 2, :], tf[:, 1, :]))
            a, b = 2, 3
            d = 1
            while d < E1:
                dve.tensor_copy(tf[:, b, 0:d], tf[:, a, 0:d])
                link(dve.tensor_tensor(tf[:, b, d:E1], tf[:, a, d:E1], tf[:, a, 0:E1 - d], ALU.add))
                a, b = b, a
                d *= 2
            one = slice(0, 1)
            link(dve.tensor_tensor(
                ge[:, :, :], iota_s[:, :].rearrange("p (s a) -> p s a", a=1).broadcast_to([1, NS, E1]),
                tf[one, a, :].rearrange("p (a e) -> p a e", a=1).broadcast_to([1, NS, E1]), ALU.is_ge))
            link(dve.tensor_reduce(ts[:, 0, :], ge[:, :, :], AX.X, ALU.add))
            link(dve.tensor_tensor(
                ge[:, :, :], ge[:, :, :],
                tf[one, 1, :].rearrange("p (a e) -> p a e", a=1).broadcast_to([1, NS, E1]), ALU.mult))
            link(dve.tensor_reduce(ts[:, 1, :], ge[:, :, :], AX.X, ALU.add))
            link(dve.tensor_tensor(ts[:, 2, :], iota_s[:, :], ts[:, 1, :], ALU.subtract))
            link(dve.tensor_scalar(ts[:, 2, :], ts[:, 2, :], float(P), None, ALU.mult))
            link(dve.tensor_scalar(ts[:, 3, :], ts[:, 0, :], float(REGION), None, ALU.mult))
            dve.tensor_tensor(tile_row[:, :], ts[:, 3, :], ts[:, 2, :], ALU.add).then_inc(s["tables"], 1)
            dve.tensor_copy(tile_e[:, :], ts[:, 0, :]).then_inc(s["tables"], 1)

            with dve.Fori(0, NE) as e:
                dve.wait_ge(s["wd_hi"], e + 1)
                low(wd_lo[:, bass.ds(2 * e, 2), :], wd_raw[:, bass.ds(2 * e, 2), :],
                    wd_hi[:, bass.ds(2 * e, 2), :], "wd_lo")

            def index(u, p):
                return V * u + p if isinstance(u, int) else None

            def product_z(t, i, p):
                dve.wait_ge(s["silu"], t + 1)
                if i is None or i >= 2:
                    dve.wait_ge(s["zT_mm"], t - 1)
                dve.tensor_tensor(z[:, p % 2, :], sg[:, p % 2, :], b_gu[p % 2][:, I1:GU], ALU.mult)\
                    .then_inc(s["z_ready"], 1)

            def zT_low(t, i, p):
                dve.wait_ge(s["zT_hi"], t + 1)
                if i is None or i >= 2:
                    dve.wait_ge(s["y_mm"], t - 1)
                low(zT_lo[:, p % 2, :, :].rearrange("p c t -> p (c t)"), b_zT[:, 0:I1],
                    zT_hi[:, p % 2, :, :].rearrange("p c t -> p (c t)"), "zT_lo")

            def spread(u, p, base):
                t = base + V * u + p
                dve.wait_ge(row_in[p], 16 * (base // V + u) + 16)
                if base or late(u, p, V, 2):
                    dve.wait_ge(s["qx_mm"], t - 1)
                dve.scalar_tensor_tensor(
                    out=qx[:, p % 2, :, :], in0=iota_a[:, :, :], scalar=row_t[:, p, A_COL:A_COL + 1],
                    in1=row_t[:, p:p + 1, 0:R].broadcast_to([P, NA, R]), op0=ALU.is_equal, op1=ALU.mult)\
                    .then_inc(s["qx_ready"], 1)

            def tile_step(u, p):
                if live(u, p, V, NS):
                    product_z(V * u + p, index(u, p), p)
                v, w = back(u, p, 1, V)
                if live(v, w, V, NS):
                    zT_low(V * v + w, index(v, w), w)
                v, w = back(u, p, -2, V)
                if live(v, w, V, NS):
                    spread(v, w, 0)
                v, w = back(u, p, 2, V)
                if live(v, w, V, NS):
                    if late(v, w, V, U):
                        dve.wait_ge(added[w % U], 16 * (V // U * v + w // U))
                    dve.wait_ge(s["y_ready"], V * v + w + 1)
                    dve.tensor_copy(tok_i[:, w % U:w % U + 1], row_t[:, w, T_COL:T_COL + 1]).then_inc(s["tok_ready"], 1)

            passes(dve, V, NS, 2, 2, tile_step)

            def last_step(u, p):
                if live(u, p, V, NT):
                    product_z(NS + V * u + p, None, p)
                v, w = back(u, p, 1, V)
                if live(v, w, V, NT):
                    zT_low(NS + V * v + w, None, w)
                v, w = back(u, p, -2, V)
                if live(v, w, V, NT):
                    spread(v, w, NS)
                v, w = back(u, p, 2, V)
                if live(v, w, V, NT):
                    t = V * v + w
                    dve.wait_ge(s["y_mm"], NS + t + 1)
                    dve.wait_ge(a_in[w], 16 * ACC * (v + 1))
                    dve.tensor_tensor(sums[:, 2 * w + 1, :], sums[:, 2 * w + 1, :], b_y[w % 2][:, :], ALU.add)\
                        .then_inc(s["sum_step"], 1)
                    dve.wait_ge(s["sum_step"], t + 1)
                    dve.tensor_tensor(sums[:, 2 * w, :], sums[:, 2 * w, :], sums[:, 2 * w + 1, :], ALU.add)\
                        .then_inc(s["out_ready"], 1)

            passes(dve, V, NT, 2, 2, last_step)


def kernel(x, itok_B_0_15, itok_B_3_7, L0_cond_weights, L0_ffn_W_base, L0_ffn_b_base, L0_ffn_W_gate, L0_ffn_A,
           L0_ffn_B, L1_cond_A, L1_cond_B, L1_ffn_gate_w, L1_ffn_bias, L1_ffn_Wg, L1_ffn_Wu, L1_ffn_Wd,
           L1_ffn_Sg, L1_ffn_Su, L1_ffn_Sd):
    import numpy as np
    import concourse.bacc as bacc
    from concourse.bass_utils import run_bass_kernel_spmd

    def arr(a):
        return np.asarray(a)

    def chunks(wt):
        return wt.reshape(KC, P, -1).transpose(1, 0, 2)

    gate0, a0 = arr(L0_ffn_W_gate), arr(L0_ffn_A).reshape(E0 * R, D)
    wg = np.concatenate([arr(L1_ffn_Wg), arr(L1_ffn_Sg)[None]])
    wu = np.concatenate([arr(L1_ffn_Wu), arr(L1_ffn_Su)[None]])
    gu = np.concatenate([wg, wu], axis=1)
    wd = np.concatenate([arr(L1_ffn_Wd), arr(L1_ffn_Sd)[None]])
    arrays = {
        "x": arr(x),
        "cond": arr(itok_B_0_15).reshape(NT, BPT).T,
        "adapters": arr(itok_B_3_7).reshape(NT, BPT).T,
        "cond_w": arr(L0_cond_weights).reshape(-1, SEQ),
        "base_w": chunks(arr(L0_ffn_W_base).T),
        "base_b": arr(L0_ffn_b_base),
        "gate_lora0": chunks(np.concatenate([gate0, a0]).T),
        "lora_b0": arr(L0_ffn_B).transpose(0, 2, 1).reshape(E0 * R, D),
        "adapter_b": chunks(arr(L1_cond_B).reshape(NA * R, D).T),
        "adapter_a": chunks(arr(L1_cond_A).transpose(1, 0, 2).reshape(D, NA * R)),
        "gate1": chunks(arr(L1_ffn_gate_w).T),
        "bias1": arr(L1_ffn_bias),
        "gate_up": gu.reshape(NE, GU, KC, P).transpose(0, 3, 2, 1),
        "down": wd.transpose(2, 0, 1).reshape(IC, P, NE, D).transpose(1, 2, 0, 3).reshape(P, NE * IC, D),
    }
    nc = bacc.Bacc("TRN2", target_bir_lowering=False, num_devices=1)
    arrays = {f"in_{n}": np.ascontiguousarray(a) for n, a in arrays.items()}
    args = [nc.dram_tensor(n, a.shape, mybir.dt.from_np(a.dtype), kind="ExternalInput").ap()
            for n, a in arrays.items()]
    args.append(nc.dram_tensor("out_0", (BATCH, SEQ, D), F32, kind="ExternalOutput").ap())
    adaln_ffn_kernel(nc, *args)
    r = run_bass_kernel_spmd(nc, [arrays], core_ids=[0])
    return r.results[0]["out_0"]
```

```python
from contextlib import ExitStack

import concourse.bass as bass
from concourse import mybir

F32 = mybir.dt.float32
F32R = mybir.dt.float32r
I32 = mybir.dt.int32
U32 = mybir.dt.uint32
ALU = mybir.AluOpType
ACT = mybir.ActivationFunctionType
AX = mybir.AxisListType

P = 128
BATCH, SEQ, D = 128, 32, 512
TOK = BATCH * SEQ
NT = TOK // P
BPT = P // SEQ
KC = D // P
E0, K0, R = 8, 2, 16
E1, K1, I1 = 16, 4, 256
IC = I1 // P
NE = E1 + 1
NA = 8
GU = 2 * I1
REGION = TOK + P
SPARE = E1
NS = TOK * K1 // P + SPARE
ROWS = E1 * REGION + SPARE * P
U = 4
V = 8
ROW = R + 4
A_COL, W_COL, T_COL = R, R + 1, R + 2
POOL_LOW = 3
AHEAD = 5


def adaln_ffn_kernel(nc, x, cond, adapters, batch_adapters, cond_w, base_w, base_b, gate_lora0, lora_b0, adapter_b,
                     adapter_a, gate1, bias1, gate_up, down, out):
    q_rows = nc.dram_tensor("q_rows", [ROWS, ROW], F32).ap()
    t_rows = nc.dram_tensor("t_rows", [TOK, ROW], F32).ap()
    acc = nc.dram_tensor("acc", [TOK + (1 + U) * P, D], F32).ap()
    xr = x.rearrange("b s d -> (b s) d")
    outr = out.rearrange("b s d -> (b s) d")

    with ExitStack() as ctx:
        def sb(name, shape, dt=F32):
            return ctx.enter_context(nc.sbuf_tensor(name, shape, dt))

        def sem(name):
            return ctx.enter_context(nc.semaphore(name))

        bank = [ctx.enter_context(nc.psum_tensor(f"bank{i}", [P, 512], F32)) for i in range(8)]

        ident = sb("ident", [P, P])
        ones = sb("ones", [P, P])
        iota_a = sb("iota_a", [P, NA, R])
        pad_row = sb("pad_row", [P, 1 + U, ROW])
        part_i = sb("part_i", [P, 1], I32)
        tile_e = sb("tile_e", [1, NS], I32)
        tile_row = sb("tile_row", [1, NS], I32)
        tile_new = sb("tile_new", [1, NS], I32)
        m_all = sb("m_all", [P, NE, GU])
        aa_sb = sb("aa_sb", [P, KC, NA * R])
        row_t = sb("row_t", [P, V, ROW])
        qx = sb("qx", [P, 2, NA, R])
        tf = sb("tf", [P, 6, E1])
        ti = sb("ti", [P, 2, E1], I32)
        pad_i = sb("pad_i", [P, E1], U32)

        first_use = ExitStack()

        def sb1(name, shape, dt=F32):
            return first_use.enter_context(nc.sbuf_tensor(name, shape, dt))

        wd_raw = sb1("wd_raw", [P, NE * IC, D])

        stage = [sb1(f"stage{b}", [P, KC, GU])[:, :, :] for b in range(2)]
        with nc.sbuf_tensor("base_w_hi", [P, KC, D], F32R) as base_w_hi:
            pass
        stage.append(sb1("stage2", [P, KC, GU])[:, :, :])
        zero_tile = sb1("zero_tile", [P, D])
        tri = sb1("tri", [P, P])
        tri_r = sb1("tri_r", [P, P], F32R)
        ones_r = sb1("ones_r", [P, P], F32R)
        diag = sb1("diag", [P, BPT, SEQ])
        iota_e = sb1("iota_e", [P, E1])
        part_f = sb1("part_f", [P, 1])
        region_f = sb1("region_f", [P, E1])
        cond_i = sb1("cond_i", [P, NT], I32)
        cond_row = sb1("cond_row", [P, NT], U32)
        c_i = sb1("c_i", [P, 1], I32)
        c_f = sb1("c_f", [P, 1])
        adapter_i = sb1("adapter_i", [P, NT], I32)
        head = sb1("head", [P, NT, ROW - R])
        base_w_lo = sb1("base_w_lo", [P, KC, D], F32R)
        base_b_sb = sb1("base_b_sb", [P, D])
        gl0_sb = sb1("gl0_sb", [P, KC, E0 + E0 * R])
        lb0_sb = sb1("lb0_sb", [P, D])
        lb0_hi = sb1("lb0_hi", [P, D], F32R)
        lb0_lo = sb1("lb0_lo", [P, D], F32R)
        ab_sb = sb1("ab_sb", [P, KC, NA * R])
        g1_sb = sb1("g1_sb", [P, KC, E1])
        gate_q = sb1("gate_q", [P, E1 + R])
        own_i = sb1("own_i", [P, 1], I32)
        own = sb1("own", [P, 1])
        batch_i = sb1("batch_i", [P, BATCH], I32)
        batch_a = sb1("batch_a", [P, BATCH])
        bias_sb = sb1("bias_sb", [P, E1])

        xt = sb1("xt", [P, U, D])
        cidx = sb1("cidx", [P, U], U32)
        wrow = sb1("wrow", [P, U, SEQ])
        bd = sb1("bd", [P, 2, BPT, SEQ])
        yT = sb1("yT", [P, 2, KC, P])
        yT_hi = sb1("yT_hi", [P, 2, KC, P], F32R)
        yT_lo = sb1("yT_lo", [P, 2, KC, P], F32R)
        hw = sb1("hw", [P, E0, R])
        hwT_hi = sb1("hwT_hi", [P, P], F32R)
        hwT_lo = sb1("hwT_lo", [P, P], F32R)
        x1 = sb1("x1", [P, U, D])
        x1T = sb1("x1T", [P, KC, P])
        qT = sb1("qT", [P, 2, P])
        rows = sb1("rows", [P, U, K1, ROW])
        slot_i = sb1("slot_i", [P, U, K1], U32)
        top0 = sb1("top0", [P, 8])
        top0_i = sb1("top0_i", [P, 8], U32)
        d0 = sb1("d0", [P, K0])
        exp0 = sb1("exp0", [P, K0])
        sum0 = sb1("sum0", [P, 2])
        oh0 = sb1("oh0", [P, K0, E0])
        ohe0 = sb1("ohe0", [P, K0, E0])
        w0 = sb1("w0", [P, E0])
        exp1 = sb1("exp1", [P, E1])
        score = sb1("score", [P, 3, E1])
        top1 = sb1("top1", [P, 8])
        top1_i = sb1("top1_i", [P, 8], U32)
        sum1 = sb1("sum1", [P, 3])
        oh = sb1("oh", [P, K1, E1])
        ohr = sb1("ohr", [P, K1, E1])
        slot_f = sb1("slot_f", [P, K1])
        mask = sb1("mask", [P, 2, E1], F32R)
        rk = sb1("rk", [P, E1])
        rowno = sb1("rowno", [P, E1])

        iota_s = sb1("iota_s", [1, NS])
        ge = sb1("ge", [1, NS, E1])
        ts = yT[0:1, :, :, :].rearrange("p s c t -> p (s c t)")[:, 0:4 * NS].rearrange("p (a n) -> p a n", a=4)
        first_use.close()

        wd_lo = sb("wd_lo", [P, NE * IC, D], F32R)
        tok_i = sb("tok_i", [P, U], U32)
        m_tile = sb("m_tile", [P, 2, GU])
        qxT = sb("qxT", [P, 2, P])
        sg = sb("sg", [P, 2, I1])
        z = sb("z", [P, 2, I1])
        z_hi = sb("z_hi", [P, 2, IC, P], F32R)
        z_lo = sb("z_lo", [P, 2, IC, P], F32R)
        y_sb = sb("y_sb", [P, U, D])
        behind = 3 * KC * GU - U - 2 * (P + 2 * I1 + 2 * IC * P + GU) - U * D
        sb("behind", [P, behind])
        wd_hi = sb("wd_hi", [P, NE * IC, D], F32R)
        sums = m_all[:, 0:V, :]

        s = {n: sem(n) for n in (
            "made", "consts", "cond_in", "small_in", "cond_row", "gl0_in", "lb0_in", "ab_in", "aa_in",
            "split_hi", "split_lo", "gate_q_mm", "gate_q_ready", "ci_ready", "bd_ready", "xb_ready",
            "hwT_hi", "yT_mm", "yT_ready", "yT_hi", "yT_lo", "h_mm", "d_ready", "exp0", "r0_step",
            "hw_ready", "hwT_mm",
            "hwT_lo", "base_mm", "r_mm", "x1_ready", "x1T_mm", "x1T_ready", "q_mm", "qT_ready", "s_mm", "exp1",
            "r1_step", "w_ready", "mask_ready", "rank_mm", "rank_step",
            "rank_done", "row_step", "rows_ready", "wd_in", "zeros_out",
            "m_mm", "m_ready", "t_step", "pad_ready", "tables", "pads", "spare_out", "wd_hi", "wd_lo",
            "wd_lo_pool",
            "qx_ready", "qx_mm", "qxT_ready", "gu_mm", "silu", "z_ready", "z_hi", "z_lo", "m_tile",
            "y_mm", "y_ready", "tok_ready", "out_ready",
            "dve_held", "pool_held")}

        def ring(name, n):
            return [sem(f"{name}{i}") for i in range(n)]

        x_in, w_in, x1_out, scat, t_out = (ring(n, U) for n in ("x_in", "w_in", "x1_out", "scat", "t_out"))
        st_in = ring("st_in", 3)
        base_w_in = ring("base_w_in", 2)
        row_in = ring("row_in", V)
        added = ring("added", U)
        a_in = ring("a_in", V)
        o_out = ring("o_out", V)

        Y, X1T, HT, H, R0, R1, Q, QT = bank
        RB = (R0, R1)
        FB = (H, R0, R1)
        EARLY = {NT - 4: 0, NT - 3: 1, NT - 1: 2, NT: 3, NT + 1: 4, NT + 2: 5, NT + 3: 6}
        rank_ps = HT[:, P:P + 2 * E1]
        s_ps, q_ps = QT[:, 0:E1], QT[:, E1:E1 + R]
        b_qx, b_gu, b_y = Y, (X1T, HT), (Q, QT, R0, R1)

        def back(u, p, lag, n):
            d = p - lag
            return u + d // n, d % n

        def live(u, p, n, count):
            return not isinstance(u, int) or 0 <= n * u + p < count

        def late(u, p, n, k):
            return not isinstance(u, int) or n * u + p >= k

        def adds(u, p):
            return 16 * (V // U * u + p // U) + 16

        def passes(eng, n, count, lag, lead, body, most_lead=None, after_lead=None, start=None):
            first = -(-(lag + n) // n)
            last = (count - (lead if most_lead is None else most_lead)) // n
            for i in range(-lead if start is None else start, first * n):
                body(i // n, i % n)
                if i == 0 and after_lead:
                    after_lead()
            with eng.Fori(first, last) as u:
                for p in range(n):
                    body(u, p)
            for i in range(last * n, count + lag):
                body(i // n, i % n)

        def stage_of(e):
            if e < 4:
                return e % 2, 16 * (e // 2) + 16
            b = (e + 1) % 3
            return b, 16 * ((e + 1) // 3) + (0 if b == 2 else 16)

        block = ctx.enter_context(nc.Block())

        @block.sync
        def _(sp):

            def step(u, p):
                t = U * u + p
                if live(u, p, U, NT):
                    if late(u, p, U, U):
                        sp.wait_ge(s["x1_ready"], t - U + 1)
                    sp.dma_start(xt[:, p, :], xr[bass.ts(t, P), :]).then_inc(x_in[p], 16)
                    if isinstance(u, int) and t == 0:
                        sp.dma_start(gl0_sb[:, :, :], gate_lora0).then_inc(s["gl0_in"], 16)
                        sp.wait_ge(s["cond_in"], 16 * BPT)
                        for n in range(2):
                            half = slice(n * KC // 2, (n + 1) * KC // 2)
                            sp.dma_start(stage[1][:, half, :], base_w[:, half, :]).then_inc(base_w_in[n], 16)
                    if isinstance(u, int) and t == 1:
                        sp.dma_start(lb0_sb[:, :], lora_b0).then_inc(s["lb0_in"], 16)
                        sp.dma_start(ab_sb[:, :, :], adapter_b).then_inc(s["ab_in"], 16)
                        sp.dma_start(aa_sb[:, :, :], adapter_a).then_inc(s["aa_in"], 16)
                        sp.dma_start(g1_sb[:, :, :], gate1).then_inc(s["aa_in"], 16)
                        sp.wait_ge(s["made"], 7)
                        sp.dma_start(acc[TOK:TOK + P, :], zero_tile[:, :]).then_inc(s["zeros_out"], 16)
                        sp.wait_ge(s["consts"], 5)
                        for n in range(SPARE):
                            sp.dma_start(q_rows[E1 * REGION + n * P:E1 * REGION + (n + 1) * P, :],
                                         pad_row[:, 1 + n % U, :]).then_inc(s["spare_out"], 16)
                    if isinstance(u, int) and t == U - 1:
                        sp.wait_ge(s["split_lo"], 2)
                        sp.wait_ge(s["split_hi"], 2)
                        for b in range(2):
                            sp.dma_start(stage[b], gate_up[b]).then_inc(st_in[b], 16)
                v, w = back(u, p, 2, U)
                if live(v, w, U, NT):
                    sp.dma_start(wd_raw[:, bass.ds(U * v + w, 1), :], down[:, bass.ds(U * v + w, 1), :])\
                        .then_inc(s["wd_in"], 16)
                v, w = back(u, p, 6, U)
                if live(v, w, U, NT):
                    sp.wait_ge(s["x1_ready"], U * v + w + 1)
                    sp.dma_start(acc[bass.ts(U * v + w, P), :], x1[:, w, :]).then_inc(x1_out[w], 16)
                    sp.wait_ge(s["w_ready"], U * v + w + 1)
                    sp.dma_start(t_rows[bass.ts(U * v + w, P), :], rows[:, w, 0, :]).then_inc(t_out[w], 16)

            passes(sp, U, NT, 6, 0, step)
            for n in range(NT, NE * IC):
                sp.dma_start(wd_raw[:, n, :], down[:, n, :]).then_inc(s["wd_in"], 16)

            with sp.Fori(4, (NE + 1) // 3) as u:
                for b in range(3):
                    sp.wait_ge(s["m_mm"], 3 * u + b - 3)
                    sp.dma_start(stage[b], gate_up[3 * u + b - 1]).then_inc(st_in[b], 16)

            sp.wait_ge(s["tables"], 3)
            sp.wait_ge(s["pads"], 16 * E1)
            sp.wait_ge(s["spare_out"], 16 * SPARE)
            for p in range(U):
                sp.wait_ge(scat[p], 16 * K1 * (NT // U))
                sp.wait_ge(t_out[p], 16 * (NT // U))

            def free_row(t, u, p, n):
                if late(u, p, V, V) or n:
                    sp.wait_ge(s["qx_ready"], t - V + 1)
                    sp.wait_ge(s["tok_ready"], t - V + 1)

            def tile_step(u, p):
                t = V * u + p
                free_row(t, u, p, 0)
                row = sp.value_load(tile_row[0:1, bass.ds(t, 1)], min_val=0, max_val=ROWS - P)
                sp.dma_start(row_t[:, p, :], q_rows[bass.ds(row, P), :]).then_inc(row_in[p], 16)

            passes(sp, V, NS, 0, 0, tile_step)

            def load_shared(u, p):
                t = V * u + p
                sp.wait_ge(s["qx_ready"], NS + t - V + 1)
                if isinstance(u, int) and t < V:
                    sp.wait_ge(s["tok_ready"], NS + t - V + 1)
                sp.dma_start(row_t[:, p, :], t_rows[bass.ts(t, P), :]).then_inc(row_in[p], 16)

            def load_sums(u, p):
                sp.dma_start(sums[:, p, :], acc[bass.ts(V * u + p, P), :]).then_inc(a_in[p], 16)

            def store_out(u, p):
                t = V * u + p
                sp.wait_ge(s["out_ready"], t + 1)
                sp.dma_start(outr[bass.ts(t, P), :], sums[:, p, :]).then_inc(o_out[p], 16)

            for p in range(V):
                load_shared(0, p)
            sp.wait_ge(s["gu_mm"], NS)
            for p in range(U):
                sp.wait_ge(added[p], 16 * (NS // U) + 16)

            def last_step(u, p):
                v, w = back(u, p, 1 - V, V)
                if live(v, w, V, NT) and late(u, p, V, 1):
                    load_shared(v, w)
                v, w = back(u, p, -AHEAD, V)
                if live(v, w, V, NT):
                    if late(v, w, V, V):
                        sp.wait_ge(o_out[w], 16 * v)
                    load_sums(v, w)
                v, w = back(u, p, 1, V)
                if live(v, w, V, NT):
                    store_out(v, w)

            passes(sp, V, NT, 1, AHEAD, last_step, V)
            for p in range(V):
                sp.wait_ge(o_out[p], 16 * (NT // V))

        @block.gpsimd
        def _(pool):
            def fill(dst, **how):
                return pool.iota(dst, allow_small_or_imprecise_dtypes=True, **how)

            pool.iota(part_i[:, :], pattern=[[0, 1]], base=0, channel_multiplier=1).then_inc(s["made"], 1)
            pool.memset(ident[:, :], 0.0).then_inc(s["made"], 1)
            pool.memset(ones[:, :], 1.0).then_inc(s["made"], 1)
            pool.memset(head[:, :, :], 0.0).then_inc(s["made"], 1)
            pool.memset(pad_row[:, :, :], 0.0).then_inc(s["made"], 1)
            pool.memset(zero_tile[:, :], 0.0).then_inc(s["made"], 1)
            fill(iota_e[:, :], pattern=[[1, E1]], base=0, channel_multiplier=0).then_inc(s["made"], 1)
            pool.wait_ge(s["made"], 7)
            pool.affine_select(out=diag[:, :, :], in_=ones[:, :].rearrange("p (b d) -> p b d", b=BPT),
                               compare_op=ALU.is_ge, fill=0.0, base=0, pattern=[[-SEQ, BPT], [0, SEQ]],
                               channel_multiplier=1).then_inc(s["consts"], 1)
            pool.wait_ge(s["consts"], 1)
            pool.affine_select(out=diag[:, :, :], in_=diag[:, :, :], compare_op=ALU.is_ge, fill=0.0,
                               base=SEQ - 1, pattern=[[SEQ, BPT], [0, SEQ]],
                               channel_multiplier=-1).then_inc(s["consts"], 1)
            pool.affine_select(out=ident[:, :], in_=ident[:, :], compare_op=ALU.not_equal, fill=1.0, base=0,
                               pattern=[[-1, P]], channel_multiplier=1).then_inc(s["consts"], 1)
            fill(pad_row[:, :, T_COL], pattern=[[P, 1 + U]], base=TOK, channel_multiplier=1)\
                .then_inc(s["consts"], 1)
            fill(head[:, :, T_COL - R], pattern=[[P, NT]], base=0, channel_multiplier=1).then_inc(s["consts"], 1)
            pool.wait_ge(s["cond_row"], 1)

            def gather_cond(u, p):
                if late(u, p, U, U):
                    pool.wait_ge(s["bd_ready"], U * u + p - U + 1)
                pool.tensor_copy(cidx[:, p:p + 1], cond_row[:, bass.ds(U * u + p, 1)]).then_inc(s["ci_ready"], 1)
                pool.wait_ge(s["ci_ready"], U * u + p + 1)
                pool.sem_inc(s["pool_held"])
                pool.indirect_dma_start(
                    out=wrow[:, p, :], out_offset=None, in_=cond_w,
                    in_offset=bass.IndirectOffsetOnAxis(ap=cidx[:, p:p + 1], axis=0)).then_inc(w_in[p], 16)

            def step(u, p):
                v, w = back(u, p, -1, U)
                if live(v, w, U, NT):
                    gather_cond(v, w)
                if isinstance(u, int) and U * u + p == -1:
                    fill(iota_a[:, :, :], pattern=[[1, NA], [0, R]], base=0, channel_multiplier=0)\
                        .then_inc(s["consts"], 1)
                    fill(region_f[:, :], pattern=[[REGION, E1]], base=0, channel_multiplier=0)\
                        .then_inc(s["consts"], 1)
                    fill(iota_s[:, :], pattern=[[1, NS]], base=0, channel_multiplier=0).then_inc(s["consts"], 1)
                    pool.affine_select(out=tri[:, :], in_=ones[:, :], compare_op=ALU.is_gt, fill=0.0, base=0,
                                       pattern=[[1, P]], channel_multiplier=-1).then_inc(s["consts"], 1)
                if isinstance(u, int) and U * u + p == U:
                    for n in range(U):
                        pool.dma_start(acc[TOK + (n + 1) * P:TOK + (n + 2) * P, :], zero_tile[:, :])\
                            .then_inc(added[n], 16)
                if live(u, p, U, NT):
                    t = U * u + p
                    pool.wait_ge(w_in[p], 16 * u + 16)
                    if late(u, p, U, 2):
                        pool.wait_ge(s["yT_mm"], t - 1)
                    pool.tensor_tensor(bd[:, p % 2, :, :], wrow[:, p:p + 1, :].broadcast_to([P, BPT, SEQ]),
                                       diag[:, :, :], ALU.mult).then_inc(s["bd_ready"], 1)
                v, w = back(u, p, 7, U)
                if live(v, w, U, NT):
                    pool.wait_ge(s["w_ready"], U * v + w + 1)
                    pool.wait_ge(s["rank_step"], 4 * (U * v + w + 1))
                    pool.sem_inc(s["pool_held"])
                    for k in range(K1):
                        pool.indirect_dma_start(
                            out=q_rows, out_offset=bass.IndirectOffsetOnAxis(ap=slot_i[:, w, k:k + 1], axis=0),
                            in_=rows[:, w, k, :], in_offset=None).then_inc(scat[w], 16)

            passes(pool, U, NT, 7, 1, step)
            pool.wait_ge(s["pad_ready"], 1)
            for e in range(E1):
                pool.indirect_dma_start(
                    out=q_rows, out_offset=bass.IndirectOffsetOnAxis(ap=pad_i[:, e:e + 1], axis=0),
                    in_=pad_row[:, 0, :], in_offset=None).then_inc(s["pads"], 16)
            for e in range(NE - POOL_LOW, NE):
                pool.wait_ge(s["wd_hi"], e + 1)
                pool.tensor_tensor(wd_lo[:, 2 * e:2 * e + 2, :], wd_raw[:, 2 * e:2 * e + 2, :],
                                   wd_hi[:, 2 * e:2 * e + 2, :].bitcast(F32), ALU.subtract)\
                    .then_inc(s["wd_lo_pool"], 1)
            pool.wait_ge(s["tables"], 3)
            for p in range(U):
                pool.wait_ge(x1_out[p], 16 * (NT // U))
            pool.wait_ge(s["zeros_out"], 16)

            def add_step(u, p):
                t = V * u + p
                if late(u, p, V, 1):
                    new = pool.value_load(tile_new[0:1, bass.ds(t, 1)], min_val=0, max_val=16)
                for d in range(1, U):
                    v, w = back(u, p, d, V)
                    if late(u, p, V, d):
                        pool.wait_ge(added[w % U], adds(v, w) + new)
                pool.wait_ge(s["tok_ready"], t + 1)
                pool.wait_ge(s["y_ready"], t + 1)
                pool.sem_inc(s["pool_held"])
                pool.indirect_dma_start(
                    out=acc, out_offset=bass.IndirectOffsetOnAxis(ap=tok_i[:, p % U:p % U + 1], axis=0),
                    in_=y_sb[:, p % U, :], in_offset=None, compute_op=ALU.add).then_inc(added[p % U], 16)

            passes(pool, V, NS, 0, 0, add_step)

        @block.scalar
        def _(act):
            for b in range(BPT):
                act.dma_start(cond_i[b * SEQ:(b + 1) * SEQ, :], cond[b:b + 1, :].broadcast_to([SEQ, NT]))\
                    .then_inc(s["cond_in"], 16)
            act.wait_ge(s["cond_in"], 16 * BPT)
            for b in range(BPT):
                act.dma_start(adapter_i[b * SEQ:(b + 1) * SEQ, :], adapters[b:b + 1, :].broadcast_to([SEQ, NT]))\
                    .then_inc(s["small_in"], 16)
            act.dma_start(base_b_sb[:, :], base_b.rearrange("(a d) -> a d", a=1).broadcast_to([P, D]))\
                .then_inc(s["small_in"], 16)
            act.dma_start(bias_sb[:, :], bias1.rearrange("(a d) -> a d", a=1).broadcast_to([P, E1]))\
                .then_inc(s["small_in"], 16)
            act.dma_start(batch_i[:, :], batch_adapters.rearrange("(a d) -> a d", a=1).broadcast_to([P, BATCH]))\
                .then_inc(s["small_in"], 16)

            def load_stage(e):
                b = stage_of(e)[0]
                act.dma_start(stage[b], gate_up[e]).then_inc(st_in[b], 16)

            def fold(e):
                act.wait_ge(s["m_mm"], e + 1)
                act.copy(m_all[:, e, :], (H if e < 3 else FB[e % 3])[:, :]).then_inc(s["m_ready"], 1)

            def step(u, p):
                i = U * u + p if isinstance(u, int) else None
                if i == NT:
                    act.wait_ge(s["base_mm"], NT)
                    load_stage(4)
                if i is not None and i > NT:
                    fold(EARLY[i - 1])
                    load_stage(EARLY[i - 1] + 3)
                v, w = back(u, p, 1, U)
                if live(v, w, U, NT):
                    t = U * v + w
                    act.wait_ge(s["hwT_mm"], t + 1)
                    if late(v, w, U, 1):
                        act.wait_ge(s["r_mm"], t)
                    act.copy(hwT_hi[:, :], HT[:, 0:P]).then_inc(s["hwT_hi"], 1)
                if live(u, p, U, NT):
                    act.wait_ge(s["d_ready"], U * u + p + 1)
                    act.activation(exp0[:, :], d0[:, :], ACT.Exp, accum_out=sum0[:, 0:1]).then_inc(s["exp0"], 1)
                v, w = back(u, p, -1, U)
                if live(v, w, U, NT):
                    t = U * v + w
                    act.wait_ge(s["yT_mm"], t + 1)
                    if late(v, w, U, 2):
                        act.wait_ge(s["base_mm"], t - 1)
                    act.copy(yT[:, w % 2, :, :].rearrange("p c t -> p (c t)"), Y[:, :]).then_inc(s["yT_ready"], 1)
                    act.copy(yT_hi[:, w % 2, :, :].rearrange("p c t -> p (c t)"), Y[:, :]).then_inc(s["yT_hi"], 1)
                if i == -1:
                    for n in range(2):
                        half = slice(n * KC // 2, (n + 1) * KC // 2)
                        act.wait_ge(base_w_in[n], 16)
                        act.copy(base_w_hi[:, half, :], stage[1][:, half, :]).then_inc(s["split_hi"], 1)
                v, w = back(u, p, 2, U)
                if live(v, w, U, NT):
                    t = U * v + w
                    act.wait_ge(s["x1T_mm"], t + 1)
                    if late(v, w, U, 1):
                        act.wait_ge(s["q_mm"], t)
                    act.copy(x1T[:, :, :].rearrange("p c t -> p (c t)"), X1T[:, :]).then_inc(s["x1T_ready"], 1)
                if i in EARLY and i < NT:
                    fold(EARLY[i])
                    load_stage((2, 3, 5)[EARLY[i]])
                v, w = back(u, p, 3, U)
                if live(v, w, U, NT):
                    t = U * v + w
                    act.wait_ge(s["s_mm"], t + 1)
                    if late(v, w, U, 1):
                        act.wait_ge(s["mask_ready"], t)
                    act.activation(exp1[:, :], s_ps, ACT.Exp, scale=-1.0).then_inc(s["exp1"], 1)
                    if late(v, w, U, U):
                        act.wait_ge(scat[w], 16 * K1 * v)
                        act.wait_ge(t_out[w], 16 * v)
                    act.copy(rows[:, w, :, 0:R],
                             q_ps.rearrange("p (a r) -> p a r", a=1).broadcast_to([P, K1, R]))\
                        .then_inc(s["row_step"], 1)
                    act.copy(rows[:, w, :, R:ROW], head[:, bass.ds(t, 1), :].broadcast_to([P, K1, ROW - R]))\
                        .then_inc(s["rows_ready"], 1)

            def first_gate():
                act.wait_ge(s["gate_q_mm"], 1)
                act.copy(gate_q[:, 0:E1], Q[:, 0:E1]).then_inc(s["gate_q_ready"], 1)

            passes(act, U, NT, 3, 1, step, after_lead=first_gate)

            def high(e):
                act.copy(wd_hi[:, bass.ds(2 * e, 2), :], wd_raw[:, bass.ds(2 * e, 2), :]).then_inc(s["wd_hi"], 1)

            for e in (5, 6, 7):
                fold(e)
                load_stage(e + 3)
            act.wait_ge(s["wd_in"], 16 * NE * IC)
            act.wait_ge(s["pad_ready"], 1)
            act.wait_ge(s["t_step"], 12)
            act.wait_ge(s["zeros_out"], 16)
            for p in range(U):
                act.wait_ge(added[p], 16)
            act.wait_ge(s["row_step"], NT)
            act.wait_ge(s["rows_ready"], NT)
            for p in range(U):
                act.wait_ge(scat[p], 16 * K1 * (NT // U))
                act.wait_ge(x1_out[p], 16 * (NT // U))
                act.wait_ge(t_out[p], 16 * (NT // U))
            for e in range(8, E1):
                fold(e)
                if e == 11:
                    act.wait_ge(s["tables"], 3)
                for n in range(3 * (e - 8), min(3 * (e - 8) + 3, NE)):
                    high(n)

            def silu(t, i, p):
                act.wait_ge(s["gu_mm"], t + 1)
                if i is None or i >= 2:
                    act.wait_ge(s["z_ready"], t - 1)
                act.activation(sg[:, p % 2, :], b_gu[p % 2][:, 0:I1], ACT.Silu).then_inc(s["silu"], 1)

            def z_high(t, i, p):
                act.wait_ge(s["z_ready"], t + 1)
                if i is None or i >= 2:
                    act.wait_ge(s["y_mm"], t - 1)
                act.copy(z_hi[:, p % 2, :, :].rearrange("p c t -> p (c t)"), z[:, p % 2, :]).then_inc(s["z_hi"], 1)

            def turned(t, i, p):
                act.wait_ge(s["qx_mm"], t + 1)
                if i is None or i >= 2:
                    act.wait_ge(s["gu_mm"], t - 1)
                act.copy(qxT[:, p % 2, :], b_qx[:, 0:P]).then_inc(s["qxT_ready"], 1)

            def index(u, p):
                return V * u + p if isinstance(u, int) else None

            def tile_step(u, p):
                t = V * u + p
                if live(u, p, V, NS):
                    silu(t, index(u, p), p)
                v, w = back(u, p, 1, V)
                if live(v, w, V, NS):
                    z_high(V * v + w, index(v, w), w)
                v, w = back(u, p, -1, V)
                if live(v, w, V, NS):
                    turned(V * v + w, index(v, w), w)
                if isinstance(u, int) and V * u + p == 0:
                    fold(E1)
                v, w = back(u, p, 2, V)
                if live(v, w, V, NS):
                    act.wait_ge(s["y_mm"], V * v + w + 1)
                    if late(v, w, V, U):
                        act.wait_ge(added[w % U], adds(v, w))
                    act.activation(y_sb[:, w % U, :], b_y[w % U][:, :], ACT.Copy, scale=row_t[:, w, W_COL:W_COL + 1])\
                        .then_inc(s["y_ready"], 1)

            def last_step(u, p):
                t = NS + V * u + p
                if live(u, p, V, NT):
                    silu(t, None, p)
                v, w = back(u, p, 1, V)
                if live(v, w, V, NT):
                    z_high(NS + V * v + w, None, w)
                v, w = back(u, p, -1, V)
                if live(v, w, V, NT):
                    turned(NS + V * v + w, None, w)

            def step(u, p):
                tile_step(u, p)
                i = V * u + p - NS if isinstance(u, int) else -V
                if i >= -1:
                    last_step(i // V, i % V)

            passes(act, V, NS, 2, 1, step)
            passes(act, V, NT, 1, 1, last_step, start=2)

        @block.tensor
        def _(pe):
            def mm(o, lhsT, rhs, start, stop):
                return pe.matmul(o, lhsT, rhs, start=start, stop=stop)

            def mm_split(o, left, right, start, stop):
                mm(o, left[0], right[0], start, False)
                mm(o, left[1], right[0], False, False)
                return mm(o, left[0], right[1], False, stop)

            def fold(e, bank, b, loaded):
                pe.wait_ge(st_in[b], loaded)
                for c in range(KC):
                    last = mm(bank[:, :], aa_sb[:, c, :], stage[b][:, c, :], c == 0, c == KC - 1)
                last.then_inc(s["m_mm"], 1)

            def step(u, p):
                i = U * u + p if isinstance(u, int) else None
                if i is not None and i >= NT:
                    e = EARLY[i]
                    if e == 3:
                        pe.wait_ge(s["hw_ready"], NT)
                        pe.wait_ge(s["m_ready"], 3)
                    elif e < 6:
                        pe.wait_ge(s["x1_ready"], NT - 5 + e)
                    else:
                        pe.wait_ge(s["m_ready"], e - 2)
                    fold(e, FB[e % 3], *stage_of(e))
                if live(u, p, U, NT):
                    t = U * u + p
                    pe.wait_ge(s["yT_ready"], t + 1)
                    if isinstance(u, int) and t == 0:
                        pe.wait_ge(s["gl0_in"], 16)
                    if late(u, p, U, 1):
                        pe.wait_ge(s["hw_ready"], t)
                    if i is not None and i - 1 in EARLY:
                        pe.wait_ge(s["m_ready"], EARLY[i - 1] + 1)
                    for c in range(KC):
                        last = mm(H[:, 0:E0 + E0 * R], yT[:, p % 2, c, :], gl0_sb[:, c, :], c == 0, c == KC - 1)
                    last.then_inc(s["h_mm"], 1)
                v, w = back(u, p, -1, U)
                if live(v, w, U, NT):
                    t = U * v + w
                    pe.wait_ge(x_in[w], 16 * v + 16)
                    pe.wait_ge(s["bd_ready"], t + 1)
                    if late(v, w, U, 1):
                        pe.wait_ge(s["yT_lo"], t)
                    for c in range(KC):
                        last = mm(Y[:, c * P:(c + 1) * P], xt[:, w, c * P:(c + 1) * P],
                                  bd[:, w % 2, :, :].rearrange("p b d -> p (b d)"), True, True)
                    last.then_inc(s["yT_mm"], 1)
                v, w = back(u, p, 1, U)
                if live(v, w, U, NT):
                    t = U * v + w
                    pe.wait_ge(s["hw_ready"], t + 1)
                    if late(v, w, U, 1):
                        pe.wait_ge(s["hwT_lo"], t)
                    if late(v, w, U, 4):
                        pe.wait_ge(s["rank_done"], t - 3)
                    pe.transpose(HT[:, 0:P], hw[:, :, :].rearrange("p e r -> p (e r)"), ident[:, :])\
                        .then_inc(s["hwT_mm"], 1)
                v, w = back(u, p, 2, U)
                if live(v, w, U, NT):
                    t = U * v + w
                    pe.wait_ge(s["x1_ready"], t + 1)
                    if late(v, w, U, 1):
                        pe.wait_ge(s["x1T_ready"], t)
                    for c in range(KC):
                        last = pe.transpose(X1T[:, c * P:(c + 1) * P], x1[:, w, c * P:(c + 1) * P], ident[:, :])
                    last.then_inc(s["x1T_mm"], 1)
                if live(u, p, U, NT):
                    t = U * u + p
                    pe.wait_ge(s["yT_lo"], t + 1)
                    if isinstance(u, int) and t == 0:
                        pe.wait_ge(s["split_hi"], 2)
                        pe.wait_ge(s["split_lo"], 2)
                    if late(u, p, U, 2):
                        pe.wait_ge(s["x1_ready"], t - 1)
                    for c in range(KC):
                        last = mm_split(RB[p % 2][:, :], (yT_hi[:, p % 2, c, :], yT_lo[:, p % 2, c, :]),
                                        (base_w_hi[:, c, :], base_w_lo[:, c, :]), c == 0, False)
                    last.then_inc(s["base_mm"], 1)
                    if i in EARLY:
                        pe.wait_ge(s["hw_ready"], t + 1)
                        fold(EARLY[i], H, *stage_of(EARLY[i]))
                v, w = back(u, p, 4, U)
                if live(v, w, U, NT):
                    t = U * v + w
                    pe.wait_ge(s["mask_ready"], t + 1)
                    pe.wait_ge(s["hwT_lo"], min(t + 4, NT) if isinstance(u, int) else t + 4)
                    mm(rank_ps[:, 0:E1], tri_r[:, :], mask[:, w % 2, :], True, True)
                    mm(rank_ps[:, E1:2 * E1], ones_r[:, :], mask[:, w % 2, :], True, True).then_inc(s["rank_mm"], 1)
                v, w = back(u, p, 3, U)
                if live(v, w, U, NT):
                    t = U * v + w
                    pe.wait_ge(s["qT_ready"], t + 1)
                    if late(v, w, U, 1):
                        pe.wait_ge(s["exp1"], t)
                        pe.wait_ge(s["row_step"], t)
                    mm(QT[:, 0:E1 + R], qT[:, w % 2, :], gate_q[:, :], True, True).then_inc(s["s_mm"], 1)
                v, w = back(u, p, 2, U)
                if live(v, w, U, NT):
                    t = U * v + w
                    pe.wait_ge(s["x1T_ready"], t + 1)
                    if isinstance(u, int) and t == 0:
                        pe.wait_ge(s["ab_in"], 16)
                        pe.wait_ge(s["gate_q_ready"], 2)
                    if late(v, w, U, 1):
                        pe.wait_ge(s["qT_ready"], t)
                    for c in range(KC):
                        last = mm(Q[:, 0:P], ab_sb[:, c, :], x1T[:, c, :], c == 0, c == KC - 1)
                    last.then_inc(s["q_mm"], 1)
                v, w = back(u, p, 1, U)
                if live(v, w, U, NT):
                    t = U * v + w
                    pe.wait_ge(s["hwT_lo"], t + 1)
                    if isinstance(u, int) and t == 0:
                        pe.wait_ge(s["split_lo"], 3)
                    mm_split(RB[w % 2][:, :], (hwT_hi[:, :], hwT_lo[:, :]), (lb0_hi[:, :], lb0_lo[:, :]),
                             False, True).then_inc(s["r_mm"], 1)

            def first_gate():
                pe.wait_ge(s["aa_in"], 32)
                for c in range(KC):
                    last = mm(Q[:, 0:E1], aa_sb[:, c, :], g1_sb[:, c, :], c == 0, c == KC - 1)
                last.then_inc(s["gate_q_mm"], 1)

            pe.wait_ge(s["consts"], 9)
            passes(pe, U, NT, 4, 1, step, after_lead=first_gate)

            pe.wait_ge(s["m_ready"], 5)
            fold(7, FB[1], *stage_of(7))
            with pe.Fori(3, NE // 3) as u:
                for b in range(3):
                    pe.wait_ge(s["m_ready"], 3 * u - 3 + b)
                    fold(3 * u - 1 + b, FB[(b + 2) % 3], b, 16 * u + (0 if b == 2 else 16))
            for e in range(NE // 3 * 3 - 1, E1):
                pe.wait_ge(s["m_ready"], e - 2)
                fold(e, FB[e % 3], *stage_of(e))

            pe.wait_ge(s["tables"], 3)
            pe.wait_ge(s["rank_done"], NT)
            pe.wait_ge(s["exp1"], NT)

            def part(tensor, e, c, n):
                if isinstance(e, int):
                    return tensor[:, n * e + c, :]
                return tensor[:, bass.ds(e * n + c, 1), :].rearrange("p a n -> p (a n)")

            def gate_up_product(t, i, p, weights):
                pe.wait_ge(s["qxT_ready"], t + 1)
                if i is None or i >= 2:
                    pe.wait_ge(s["z_ready"], t - 1)
                for c in range(2 * IC):
                    cols = slice(c * P, (c + 1) * P)
                    last = mm(b_gu[p % 2][:, cols], weights[:, cols], qxT[:, p % 2, :], True, True)
                last.then_inc(s["gu_mm"], 1)

            def turn_q(t, i, p):
                pe.wait_ge(s["qx_ready"], t + 1)
                if i is None or i >= 1:
                    pe.wait_ge(s["qxT_ready"], t)
                pe.transpose(b_qx[:, 0:P], qx[:, p % 2, :, :].rearrange("p a r -> p (a r)"), ident[:, :])\
                    .then_inc(s["qx_mm"], 1)

            def down_product(t, p, e, free):
                pe.wait_ge(s["z_lo"], t + 1)
                free()
                for c in range(IC):
                    last = mm_split(b_y[p % U][:, :], (z_hi[:, p % 2, c, :], z_lo[:, p % 2, c, :]),
                                    (part(wd_hi, e, c, IC), part(wd_lo, e, c, IC)), c == 0, c == IC - 1)
                last.then_inc(s["y_mm"], 1)

            def expert_of(t):
                return pe.value_load(tile_e[0:1, bass.ds(t, 1)], min_val=0, max_val=NE - 1)

            def index(u, p):
                return V * u + p if isinstance(u, int) else None

            def tile_step(u, p):
                v, w = back(u, p, 2, V)
                if live(v, w, V, NS):
                    e = expert_of(V * v + w)
                if live(u, p, V, NS):
                    pe.wait_ge(s["m_tile"], V * u + p + 1)
                    gate_up_product(V * u + p, index(u, p), p, m_tile[:, p % 2, :])
                v, w = back(u, p, -1, V)
                if live(v, w, V, NS):
                    turn_q(V * v + w, index(v, w), w)
                if isinstance(u, int) and V * u + p == 0:
                    pe.wait_ge(s["m_ready"], E1 - 2)
                    fold(E1, FB[E1 % 3], *stage_of(E1))
                v, w = back(u, p, 2, V)
                if live(v, w, V, NS):
                    t = V * v + w

                    def free():
                        if late(v, w, V, U):
                            pe.wait_ge(s["y_ready"], t - U + 1)
                        elif w == 0:
                            pe.wait_ge(s["m_ready"], NE)
                            pe.wait_ge(s["wd_hi"], NE)
                            pe.wait_ge(s["wd_lo"], NE - POOL_LOW)
                            pe.wait_ge(s["wd_lo_pool"], POOL_LOW)

                    down_product(t, w, e, free)

            def last_step(u, p):
                if live(u, p, V, NT):
                    gate_up_product(NS + V * u + p, None, p, m_all[:, NE - 1, :])
                v, w = back(u, p, -1, V)
                if live(v, w, V, NT):
                    turn_q(NS + V * v + w, None, w)
                v, w = back(u, p, 2, V)
                if live(v, w, V, NT):
                    t = V * v + w

                    def free():
                        if late(v, w, V, U):
                            pe.wait_ge(s["out_ready"], t - U + 1)
                        else:
                            pe.wait_ge(s["y_ready"], NS + t - U + 1)

                    down_product(NS + t, w, NE - 1, free)

            def step(u, p):
                tile_step(u, p)
                i = V * u + p - NS if isinstance(u, int) else -V
                if i >= -1:
                    last_step(i // V, i % V)

            passes(pe, V, NS, 2, 1, step)
            passes(pe, V, NT, 2, 1, last_step, start=2)

        @block.vector
        def _(dve):
            def low(out_, exact, high, what):
                dve.tensor_tensor(out_, exact, high.bitcast(F32), ALU.subtract).then_inc(s[what], 1)

            dve.wait_ge(s["made"], 4)
            dve.tensor_scalar(c_i[:, :], part_i[:, :], SEQ - 1, None, ALU.bitwise_and).then_inc(s["t_step"], 1)
            dve.tensor_scalar(own_i[:, :], part_i[:, :], R.bit_length() - 1, None, ALU.arith_shift_right)\
                .then_inc(s["t_step"], 1)
            dve.wait_ge(s["t_step"], 2)
            dve.tensor_copy(c_f[:, :], c_i[:, :]).then_inc(s["t_step"], 1)
            dve.tensor_copy(own[:, :], own_i[:, :]).then_inc(s["t_step"], 1)
            dve.tensor_copy(part_f[:, :], part_i[:, :]).then_inc(s["t_step"], 1)
            dve.wait_ge(s["cond_in"], 16 * BPT)
            dve.wait_ge(s["t_step"], 5)
            dve.tensor_scalar(cond_row[:, :], cond_i[:, :], float(SEQ), c_f[:, 0:1], ALU.mult, ALU.add)\
                .then_inc(s["cond_row"], 1)
            dve.wait_ge(s["consts"], 5)
            dve.tensor_reduce(gate_q[:, E1:E1 + R], ident[:, :].rearrange("p (a r) -> p r a", a=NA), AX.X, ALU.add)\
                .then_inc(s["gate_q_ready"], 1)
            dve.wait_ge(s["consts"], 9)
            dve.tensor_copy(rowno[:, :], region_f[:, :]).then_inc(s["t_step"], 1)
            dve.tensor_copy(tri_r[:, :], tri[:, :]).then_inc(s["t_step"], 1)
            dve.tensor_copy(ones_r[:, :], ones[:, :]).then_inc(s["t_step"], 1)
            dve.wait_ge(s["t_step"], 8)

            def later_inputs():
                dve.wait_ge(s["lb0_in"], 16)
                dve.tensor_copy(lb0_hi[:, :], lb0_sb[:, :]).then_inc(s["t_step"], 1)
                dve.wait_ge(s["small_in"], 16 * (BPT + 3))
                dve.tensor_copy(head[:, :, A_COL - R], adapter_i[:, :]).then_inc(s["t_step"], 1)
                dve.tensor_copy(batch_a[:, :], batch_i[:, :]).then_inc(s["t_step"], 1)
                dve.wait_ge(s["t_step"], 11)
                low(lb0_lo[:, :], lb0_sb[:, :], lb0_hi[:, :], "split_lo")

            def routing(zero, one, rank):
                live0, live1, live_rank = (live(*tile, U, NT) for tile in (zero, one, rank))
                (u0, p0), (u1, p1), (u2, p2) = zero, one, rank
                t0, t1, t2 = U * u0 + p0, U * u1 + p1, U * u2 + p2
                at0, at1, at2 = 6 * t0, 9 * t1, 4 * t2

                if live_rank:
                    dve.wait_ge(s["rank_mm"], t2 + 1)
                    dve.tensor_tensor(rk[:, :], rank_ps[:, 0:E1], rowno[:, :], ALU.add).then_inc(s["rank_step"], 1)
                if live1:
                    dve.wait_ge(s["exp1"], t1 + 1)
                    dve.tensor_scalar(score[:, 0, :], exp1[:, :], 1.0, None, ALU.add).then_inc(s["r1_step"], 1)
                if live_rank:
                    dve.wait_ge(s["rank_step"], at2 + 1)
                    dve.tensor_tensor(rowno[:, :], rowno[:, :], rank_ps[:, E1:2 * E1], ALU.add)\
                        .then_inc(s["rank_done"], 1)
                    dve.tensor_tensor(ohr[:, :, :], oh[:, :, :],
                                      rk[:, :].rearrange("p (a e) -> p a e", a=1).broadcast_to([P, K1, E1]),
                                      ALU.mult).then_inc(s["rank_step"], 1)
                if live1:
                    dve.wait_ge(s["r1_step"], at1 + 1)
                    dve.reciprocal(score[:, 1, :], score[:, 0, :]).then_inc(s["r1_step"], 1)
                if live0:
                    dve.wait_ge(s["h_mm"], t0 + 1)
                    dve.sem_inc(s["dve_held"])
                    dve.max(top0[:, :], H[:, 0:E0]).then_inc(s["r0_step"], 1)
                if live_rank:
                    dve.wait_ge(s["rank_step"], at2 + 2)
                    dve.tensor_reduce(slot_f[:, :], ohr[:, :, :], AX.X, ALU.add).then_inc(s["rank_step"], 1)
                if live1:
                    dve.wait_ge(s["r1_step"], at1 + 2)
                    dve.tensor_tensor(score[:, 2, :], score[:, 1, :], bias_sb[:, :], ALU.add)\
                        .then_inc(s["r1_step"], 1)
                if live0:
                    dve.wait_ge(s["r0_step"], at0 + 1)
                    dve.tensor_scalar(d0[:, :], top0[:, 0:K0], top0[:, 0:1], None, ALU.subtract)\
                        .then_inc(s["d_ready"], 1)
                    dve.sem_inc(s["dve_held"])
                    dve.max_index(top0_i[:, :], top0[:, :], H[:, 0:E0]).then_inc(s["r0_step"], 1)
                if live1:
                    if late(u1, p1, U, 1):
                        dve.wait_ge(s["w_ready"], t1)
                    dve.wait_ge(s["r1_step"], at1 + 3)
                    dve.sem_inc(s["dve_held"])
                    dve.max(top1[:, :], score[:, 2, :]).then_inc(s["r1_step"], 1)
                if live_rank:
                    if late(u2, p2, U, U):
                        dve.wait_ge(scat[p2], 16 * K1 * u2)
                    dve.wait_ge(s["rank_step"], at2 + 3)
                    dve.tensor_copy(slot_i[:, p2, :], slot_f[:, :]).then_inc(s["rank_step"], 1)
                if live0:
                    dve.wait_ge(s["r0_step"], at0 + 2)
                    dve.tensor_tensor(
                        oh0[:, :, :], iota_e[:, 0:E0].rearrange("p (a e) -> p a e", a=1).broadcast_to([P, K0, E0]),
                        top0_i[:, 0:K0].rearrange("p (k a) -> p k a", a=1).broadcast_to([P, K0, E0]),
                        ALU.is_equal).then_inc(s["r0_step"], 1)
                if live1:
                    dve.wait_ge(s["r1_step"], at1 + 4)
                    dve.sem_inc(s["dve_held"])
                    dve.max_index(top1_i[:, :], top1[:, :], score[:, 2, :]).then_inc(s["r1_step"], 1)
                    dve.tensor_reduce(sum1[:, 0:1], top1[:, 0:K1], AX.X, ALU.add).then_inc(s["r1_step"], 1)
                if live0:
                    dve.wait_ge(s["exp0"], t0 + 1)
                    dve.wait_ge(s["r0_step"], at0 + 3)
                    dve.tensor_tensor(ohe0[:, :, :], oh0[:, :, :],
                                      exp0[:, :].rearrange("p (k a) -> p k a", a=1).broadcast_to([P, K0, E0]),
                                      ALU.mult).then_inc(s["r0_step"], 1)
                    dve.reciprocal(sum0[:, 1:2], sum0[:, 0:1]).then_inc(s["r0_step"], 1)
                if live1:
                    if live_rank:
                        dve.wait_ge(s["rank_step"], at2 + 3)
                    dve.wait_ge(s["r1_step"], at1 + 6)
                    dve.tensor_tensor(
                        oh[:, :, :], iota_e[:, :].rearrange("p (a e) -> p a e", a=1).broadcast_to([P, K1, E1]),
                        top1_i[:, 0:K1].rearrange("p (k a) -> p k a", a=1).broadcast_to([P, K1, E1]),
                        ALU.is_equal).then_inc(s["r1_step"], 1)
                    dve.tensor_scalar(sum1[:, 1:2], sum1[:, 0:1], 1e-20, None, ALU.add).then_inc(s["r1_step"], 1)
                if live0:
                    dve.wait_ge(s["r0_step"], at0 + 5)
                    dve.tensor_reduce(w0[:, :], ohe0[:, :, :].rearrange("p k e -> p e k"), AX.X, ALU.add)\
                        .then_inc(s["r0_step"], 1)
                if live1:
                    dve.wait_ge(s["r1_step"], at1 + 8)
                    with nc.allow_low_precision(reason="sums of a few 0s and at most one 1 are exact"):
                        dve.tensor_reduce(mask[:, p1 % 2, :], oh[:, :, :].rearrange("p k e -> p e k"), AX.X,
                                          ALU.add).then_inc(s["mask_ready"], 1)
                    dve.reciprocal(sum1[:, 2:3], sum1[:, 1:2]).then_inc(s["r1_step"], 1)
                if live0:
                    if late(u0, p0, U, 1):
                        dve.wait_ge(s["hwT_mm"], t0)
                    dve.wait_ge(s["r0_step"], at0 + 6)
                    dve.scalar_tensor_tensor(
                        out=hw[:, :, :], in0=H[:, E0:E0 + E0 * R].rearrange("p (e r) -> p e r", e=E0),
                        scalar=sum0[:, 1:2],
                        in1=w0[:, :].rearrange("p (e a) -> p e a", a=1).broadcast_to([P, E0, R]),
                        op0=ALU.mult, op1=ALU.mult).then_inc(s["hw_ready"], 1)
                if live1:
                    dve.wait_ge(s["rows_ready"], t1 + 1)
                    dve.wait_ge(s["r1_step"], at1 + 9)
                    dve.tensor_scalar(rows[:, p1, :, W_COL], top1[:, 0:K1], sum1[:, 2:3], None, ALU.mult)\
                        .then_inc(s["w_ready"], 1)

            def step(u, p):
                v, w = back(u, p, 2, U)
                if live(v, w, U, NT):
                    dve.wait_ge(s["xb_ready"], U * v + w + 1)
                    dve.wait_ge(s["r_mm"], U * v + w + 1)
                    if late(v, w, U, U):
                        dve.wait_ge(x1_out[w], 16 * v)
                    dve.tensor_tensor(x1[:, w, :], RB[w % 2][:, :], xt[:, w, :], ALU.add)\
                        .then_inc(s["x1_ready"], 1)
                routing((u, p), back(u, p, 4, U), back(u, p, 5, U))
                v, w = back(u, p, 1, U)
                if live(v, w, U, NT):
                    dve.wait_ge(s["hwT_hi"], U * v + w + 1)
                    if late(v, w, U, 1):
                        dve.wait_ge(s["r_mm"], U * v + w)
                    low(hwT_lo[:, :], HT[:, 0:P], hwT_hi[:, :], "hwT_lo")
                    dve.wait_ge(s["yT_mm"], U * v + w + 1)
                    dve.tensor_tensor(xt[:, w, :], xt[:, w, :], base_b_sb[:, :], ALU.add).then_inc(s["xb_ready"], 1)
                v, w = back(u, p, -1, U)
                if live(v, w, U, NT):
                    dve.wait_ge(s["yT_hi"], U * v + w + 1)
                    low(yT_lo[:, w % 2, :, :].rearrange("p c t -> p (c t)"), Y[:, :],
                        yT_hi[:, w % 2, :, :].rearrange("p c t -> p (c t)"), "yT_lo")
                if isinstance(u, int) and U * u + p == -1:
                    for n in range(2):
                        half = slice(n * KC // 2, (n + 1) * KC // 2)
                        dve.wait_ge(s["split_hi"], n + 1)
                        low(base_w_lo[:, half, :], stage[1][:, half, :], base_w_hi[:, half, :], "split_lo")
                v, w = back(u, p, 2, U)
                if live(v, w, U, NT):
                    t = U * v + w
                    dve.wait_ge(s["q_mm"], t + 1)
                    if late(v, w, U, 2):
                        dve.wait_ge(s["s_mm"], t - 1)
                    dve.scalar_tensor_tensor(
                        out=qT[:, w % 2, :].rearrange("p (b d) -> p b d", b=BPT),
                        in0=batch_a[:, bass.ds(BPT * t, BPT)].rearrange("p (b a) -> p b a", a=1)
                        .broadcast_to([P, BPT, SEQ]),
                        scalar=own[:, :], in1=Q[:, 0:P].rearrange("p (b d) -> p b d", b=BPT),
                        op0=ALU.is_equal, op1=ALU.mult).then_inc(s["qT_ready"], 1)

            passes(dve, U, NT, 5, 1, step, after_lead=later_inputs)

            n = [11]

            def link(ins):
                ins.then_inc(s["t_step"], 1)
                n[0] += 1
                dve.wait_ge(s["t_step"], n[0])

            dve.wait_ge(s["rank_done"], NT)
            dve.tensor_scalar(pad_i[:, :], rowno[:, :], part_f[:, 0:1], None, ALU.add).then_inc(s["pad_ready"], 1)
            link(dve.tensor_tensor(tf[:, 0, :], rowno[:, :], region_f[:, :], ALU.subtract))
            link(dve.tensor_scalar(ti[:, 0, :], tf[:, 0, :], float(P - 1), None, ALU.add))
            link(dve.tensor_scalar(ti[:, 1, :], ti[:, 0, :], P.bit_length() - 1, None, ALU.arith_shift_right))
            link(dve.tensor_copy(tf[:, 1, :], ti[:, 1, :]))
            link(dve.tensor_copy(tf[:, 2, :], tf[:, 1, :]))
            a, b = 2, 3
            d = 1
            while d < E1:
                dve.tensor_copy(tf[:, b, 0:d], tf[:, a, 0:d])
                link(dve.tensor_tensor(tf[:, b, d:E1], tf[:, a, d:E1], tf[:, a, 0:E1 - d], ALU.add))
                a, b = b, a
                d *= 2
            one = slice(0, 1)
            link(dve.tensor_tensor(
                ge[:, :, :], iota_s[:, :].rearrange("p (s a) -> p s a", a=1).broadcast_to([1, NS, E1]),
                tf[one, a, :].rearrange("p (a e) -> p a e", a=1).broadcast_to([1, NS, E1]), ALU.is_ge))
            link(dve.tensor_reduce(ts[:, 0, :], ge[:, :, :], AX.X, ALU.add))
            link(dve.tensor_tensor(
                ge[:, :, :], ge[:, :, :],
                tf[one, 1, :].rearrange("p (a e) -> p a e", a=1).broadcast_to([1, NS, E1]), ALU.mult))
            link(dve.tensor_reduce(ts[:, 1, :], ge[:, :, :], AX.X, ALU.add))
            link(dve.tensor_tensor(ts[:, 2, :], iota_s[:, :], ts[:, 1, :], ALU.subtract))
            link(dve.tensor_scalar(ts[:, 2, :], ts[:, 2, :], float(P), None, ALU.mult))
            link(dve.tensor_scalar(ts[:, 3, :], ts[:, 0, :], float(REGION), None, ALU.mult))
            dve.tensor_tensor(tile_row[:, :], ts[:, 3, :], ts[:, 2, :], ALU.add).then_inc(s["tables"], 1)
            dve.tensor_copy(tile_e[:, :], ts[:, 0, :]).then_inc(s["tables"], 1)
            link(dve.tensor_tensor(ts[:, 1, 1:NS], ts[:, 0, 1:NS], ts[:, 0, 0:NS - 1], ALU.is_gt))
            dve.tensor_scalar(tile_new[:, 1:NS], ts[:, 1, 1:NS], 16.0, None, ALU.mult).then_inc(s["tables"], 1)

            with dve.Fori(0, NE - POOL_LOW) as e:
                dve.wait_ge(s["wd_hi"], e + 1)
                low(wd_lo[:, bass.ds(2 * e, 2), :], wd_raw[:, bass.ds(2 * e, 2), :],
                    wd_hi[:, bass.ds(2 * e, 2), :], "wd_lo")

            def index(u, p):
                return V * u + p if isinstance(u, int) else None

            def product_z(t, i, p):
                dve.wait_ge(s["silu"], t + 1)
                if i is None or i >= 2:
                    dve.wait_ge(s["z_lo"], t - 1)
                dve.tensor_tensor(z[:, p % 2, :], sg[:, p % 2, :], b_gu[p % 2][:, I1:GU], ALU.mult)\
                    .then_inc(s["z_ready"], 1)

            def z_low(t, i, p):
                dve.wait_ge(s["z_hi"], t + 1)
                if i is None or i >= 2:
                    dve.wait_ge(s["y_mm"], t - 1)
                low(z_lo[:, p % 2, :, :].rearrange("p c t -> p (c t)"), z[:, p % 2, :],
                    z_hi[:, p % 2, :, :].rearrange("p c t -> p (c t)"), "z_lo")

            def spread(u, p, base):
                t = base + V * u + p
                dve.wait_ge(row_in[p], 16 * (base // V + u) + 16)
                if base or late(u, p, V, 2):
                    dve.wait_ge(s["qx_mm"], t - 1)
                dve.scalar_tensor_tensor(
                    out=qx[:, p % 2, :, :], in0=iota_a[:, :, :], scalar=row_t[:, p, A_COL:A_COL + 1],
                    in1=row_t[:, p:p + 1, 0:R].broadcast_to([P, NA, R]), op0=ALU.is_equal, op1=ALU.mult)\
                    .then_inc(s["qx_ready"], 1)

            def fetch_weights(u, p, e):
                t = V * u + p
                if late(u, p, V, 2):
                    dve.wait_ge(s["gu_mm"], t - 1)
                else:
                    dve.wait_ge(s["m_ready"], E1)
                if isinstance(u, int) and t == U:
                    dve.wait_ge(s["m_ready"], NE)
                dve.tensor_copy(m_tile[:, p % 2, :], m_all[:, bass.ds(e, 1), :].rearrange("p a n -> p (a n)"))\
                    .then_inc(s["m_tile"], 1)

            def tile_step(u, p):
                v, w = back(u, p, -2, V)
                if live(v, w, V, NS):
                    e = dve.value_load(tile_e[0:1, bass.ds(V * v + w, 1)], min_val=0, max_val=NE - 1)
                v, w = back(u, p, 3, V)
                if live(v, w, V, NS):
                    if late(v, w, V, U):
                        dve.wait_ge(added[w % U], adds(v, w))
                    dve.wait_ge(s["y_ready"], V * v + w + 1)
                    dve.tensor_copy(tok_i[:, w % U:w % U + 1], row_t[:, w, T_COL:T_COL + 1])\
                        .then_inc(s["tok_ready"], 1)
                if live(u, p, V, NS):
                    product_z(V * u + p, index(u, p), p)
                v, w = back(u, p, 1, V)
                if live(v, w, V, NS):
                    z_low(V * v + w, index(v, w), w)
                v, w = back(u, p, -2, V)
                if live(v, w, V, NS):
                    spread(v, w, 0)
                    fetch_weights(v, w, e)

            def last_step(u, p):
                if live(u, p, V, NT):
                    product_z(NS + V * u + p, None, p)
                v, w = back(u, p, 1, V)
                if live(v, w, V, NT):
                    z_low(NS + V * v + w, None, w)
                v, w = back(u, p, -2, V)
                if live(v, w, V, NT):
                    spread(v, w, NS)
                v, w = back(u, p, U, V)
                if live(v, w, V, NT):
                    t = V * v + w
                    dve.wait_ge(s["y_mm"], NS + t + 1)
                    dve.wait_ge(a_in[w], 16 * (v + 1))
                    dve.tensor_tensor(sums[:, w, :], sums[:, w, :], b_y[w % U][:, :], ALU.add)\
                        .then_inc(s["out_ready"], 1)

            def step(u, p):
                tile_step(u, p)
                i = V * u + p - NS if isinstance(u, int) else -V
                if i >= -2:
                    last_step(i // V, i % V)

            passes(dve, V, NS, 3, 2, step)
            passes(dve, V, NT, U, 2, last_step, start=3)


def kernel(x, itok_B_0_15, itok_B_3_7, L0_cond_weights, L0_ffn_W_base, L0_ffn_b_base, L0_ffn_W_gate, L0_ffn_A,
           L0_ffn_B, L1_cond_A, L1_cond_B, L1_ffn_gate_w, L1_ffn_bias, L1_ffn_Wg, L1_ffn_Wu, L1_ffn_Wd,
           L1_ffn_Sg, L1_ffn_Su, L1_ffn_Sd):
    import numpy as np
    import concourse.bacc as bacc
    from concourse.bass_utils import run_bass_kernel_spmd

    def arr(a):
        return np.asarray(a)

    def chunks(wt):
        return wt.reshape(KC, P, -1).transpose(1, 0, 2)

    gate0, a0 = arr(L0_ffn_W_gate), arr(L0_ffn_A).reshape(E0 * R, D)
    wg = np.concatenate([arr(L1_ffn_Wg), arr(L1_ffn_Sg)[None]])
    wu = np.concatenate([arr(L1_ffn_Wu), arr(L1_ffn_Su)[None]])
    gu = np.concatenate([wg, wu], axis=1)
    wd = np.concatenate([arr(L1_ffn_Wd), arr(L1_ffn_Sd)[None]])
    arrays = {
        "x": arr(x),
        "cond": arr(itok_B_0_15).reshape(NT, BPT).T,
        "adapters": arr(itok_B_3_7).reshape(NT, BPT).T,
        "batch_adapters": arr(itok_B_3_7),
        "cond_w": arr(L0_cond_weights).reshape(-1, SEQ),
        "base_w": chunks(arr(L0_ffn_W_base).T),
        "base_b": arr(L0_ffn_b_base),
        "gate_lora0": chunks(np.concatenate([gate0, a0]).T),
        "lora_b0": arr(L0_ffn_B).transpose(0, 2, 1).reshape(E0 * R, D),
        "adapter_b": chunks(arr(L1_cond_B).reshape(NA * R, D).T),
        "adapter_a": chunks(arr(L1_cond_A).transpose(1, 0, 2).reshape(D, NA * R)),
        "gate1": chunks(arr(L1_ffn_gate_w).T),
        "bias1": arr(L1_ffn_bias),
        "gate_up": gu.reshape(NE, GU, KC, P).transpose(0, 3, 2, 1),
        "down": wd.transpose(2, 0, 1).reshape(IC, P, NE, D).transpose(1, 2, 0, 3).reshape(P, NE * IC, D),
    }
    nc = bacc.Bacc("TRN2", target_bir_lowering=False, num_devices=1)
    arrays = {f"in_{n}": np.ascontiguousarray(a) for n, a in arrays.items()}
    args = [nc.dram_tensor(n, a.shape, mybir.dt.from_np(a.dtype), kind="ExternalInput").ap()
            for n, a in arrays.items()]
    args.append(nc.dram_tensor("out_0", (BATCH, SEQ, D), F32, kind="ExternalOutput").ap())
    adaln_ffn_kernel(nc, *args)
    r = run_bass_kernel_spmd(nc, [arrays], core_ids=[0])
    return r.results[0]["out_0"]
```
